# Optimizing a Trainium2 kernel written in Bass

```python
import numpy as np
import jax
import jax.numpy as jnp

def _softmax(x, axis=-1):
    return jax.nn.softmax(x, axis=axis)

def _gelu(x):
    return jax.nn.gelu(x, approximate=True)

def _silu(x):
    return jax.nn.silu(x)

def _sigmoid(x):
    return jax.nn.sigmoid(x)

def _layernorm(x, axis=-1, eps=1e-05):
    m = jnp.mean(x, axis=axis, keepdims=True)
    v = jnp.var(x, axis=axis, keepdims=True)
    return (x - m) / jnp.sqrt(v + eps)

def _scatter_add(tgt, idx, src, axis=0):
    return tgt.at[idx].add(src)

def _segment_sum(src, seg, n):
    return jax.ops.segment_sum(src, seg, n)
kernel_name = 'mk_macaron_d1_jaxref_r8_ae60fc'

def setup_inputs(seed: int=0):
    np.random.seed(seed)
    _w = jnp.asarray

    def _L0_attn_setup():
        import jax, jax.numpy as jnp
        import numpy as np
        DIM = 128
        DIM_HEAD = 16
        HEADS = 8
        EPS = 1e-05

        def rms_norm(x, gamma):
            n = jnp.sqrt(jnp.sum(x * x, axis=-1, keepdims=True))
            return gamma * (x / jnp.maximum(n, 1e-12)) * x.shape[-1] ** 0.5

        def second_taylor_expansion(x):
            d = x.shape[-1]
            x0 = jnp.ones(x.shape[:-1] + (1,), dtype=x.dtype)
            x2 = jnp.einsum('...i,...j->...ij', x, x) * 0.5 ** 0.5
            x2 = x2.reshape(x.shape[:-1] + (d * d,))
            return jnp.concatenate([x0, x, x2], axis=-1)
        key = jax.random.key(seed)
        ks = jax.random.split(key, 4)
        b, n = (4, 1024)
        dim_inner = DIM_HEAD * HEADS
        x = jax.random.normal(ks[0], (b, n, DIM), dtype=jnp.float32)
        gamma = jnp.ones((DIM,), dtype=jnp.float32)
        w_q = jax.random.normal(ks[1], (DIM, dim_inner), dtype=jnp.float32) * DIM ** (-0.5)
        w_kv = jax.random.normal(ks[2], (DIM, dim_inner * 2), dtype=jnp.float32) * DIM ** (-0.5)
        w_out = jax.random.normal(ks[3], (dim_inner, DIM), dtype=jnp.float32) * dim_inner ** (-0.5)
        return {'x': x, 'gamma': gamma, 'w_q': w_q, 'w_kv': w_kv, 'w_out': w_out}
    _L0_attn_in = _L0_attn_setup()

    def _L0_ffn_setup():
        import jax, jax.numpy as jnp
        import numpy as np
        D, H, O, E, TOPK = (128, 512, 128, 8, 2)
        B, L = (2, 256)
        ROUTE_SCALE = 1.0
        key = jax.random.key(seed)
        ks = jax.random.split(key, 7)
        gb = float(np.sqrt(6.0 / (E + D)))
        return {'x': jax.random.normal(ks[0], (B, L, D), dtype=jnp.float32), 'gate_w': jax.random.uniform(ks[1], (E, D), jnp.float32, -gb, gb), 'gate_b': jnp.zeros((E,), jnp.float32), 'w1': jax.random.normal(ks[2], (E, D, H), jnp.float32) * 0.02, 'b1': jnp.zeros((E, H), jnp.float32), 'w2': jax.random.normal(ks[3], (E, H, O), jnp.float32) * 0.02, 'b2': jnp.zeros((E, O), jnp.float32)}
    _L0_ffn_in = _L0_ffn_setup()
    _d = {'L0_attn_x': _L0_attn_in['x'], 'L0_attn_gamma': _L0_attn_in['gamma'], 'L0_attn_w_q': _L0_attn_in['w_q'], 'L0_attn_w_kv': _L0_attn_in['w_kv'], 'L0_attn_w_out': _L0_attn_in['w_out'], 'L0_ffn_gate_w': _L0_ffn_in['gate_w'], 'L0_ffn_gate_b': _L0_ffn_in['gate_b'], 'L0_ffn_w1': _L0_ffn_in['w1'], 'L0_ffn_b1': _L0_ffn_in['b1'], 'L0_ffn_w2': _L0_ffn_in['w2'], 'L0_ffn_b2': _L0_ffn_in['b2']}
    _x0 = _d['L0_attn_x']
    _d['L0_attn_x'] = jax.random.normal(jax.random.fold_in(jax.random.key(seed), 1), (8, 512, 128), dtype=_x0.dtype)
    del _x0
    return _d

def reference(L0_attn_x, L0_attn_gamma, L0_attn_w_q, L0_attn_w_kv, L0_attn_w_out, L0_ffn_gate_w, L0_ffn_gate_b, L0_ffn_w1, L0_ffn_b1, L0_ffn_w2, L0_ffn_b2):

    def _L0_attn_ref(x, gamma, w_q, w_kv, w_out):
        import jax, jax.numpy as jnp
        import numpy as np
        DIM = 128
        DIM_HEAD = 16
        HEADS = 8
        EPS = 1e-05

        def rms_norm(x, gamma):
            n = jnp.sqrt(jnp.sum(x * x, axis=-1, keepdims=True))
            return gamma * (x / jnp.maximum(n, 1e-12)) * x.shape[-1] ** 0.5

        def second_taylor_expansion(x):
            d = x.shape[-1]
            x0 = jnp.ones(x.shape[:-1] + (1,), dtype=x.dtype)
            x2 = jnp.einsum('...i,...j->...ij', x, x) * 0.5 ** 0.5
            x2 = x2.reshape(x.shape[:-1] + (d * d,))
            return jnp.concatenate([x0, x, x2], axis=-1)
        b, n, _ = x.shape
        h, dh = (HEADS, DIM_HEAD)
        normed = rms_norm(x, gamma)
        q = (normed @ w_q).reshape(b, n, h, dh).transpose(0, 2, 1, 3)
        kv = (normed @ w_kv).reshape(b, n, 2, h, dh).transpose(2, 0, 3, 1, 4)
        k, v = (kv[0], kv[1])
        q = q * dh ** (-0.5)
        q = second_taylor_expansion(q)
        k = second_taylor_expansion(k)
        kv_state = jnp.einsum('bhnd,bhne->bhde', k, v)
        k_sum = jnp.sum(k, axis=2)
        den = jnp.einsum('bhnd,bhd->bhn', q, k_sum)
        qk_inv = 1.0 / jnp.maximum(den, EPS)
        out = jnp.einsum('bhnd,bhde->bhne', q, kv_state) * qk_inv[..., None]
        out = out.transpose(0, 2, 1, 3).reshape(b, n, h * dh)
        return out @ w_out

    def _L0_ffn_ref(x, gate_w, gate_b, w1, b1, w2, b2):
        import jax, jax.numpy as jnp
        import numpy as np
        D, H, O, E, TOPK = (128, 512, 128, 8, 2)
        B, L = (2, 256)
        ROUTE_SCALE = 1.0
        Bb, Ll, Dd = x.shape
        N = Bb * Ll
        x_flat = x.reshape(N, Dd)
        logits = x_flat @ gate_w.T + gate_b
        probs = jax.nn.softmax(logits * ROUTE_SCALE, axis=-1)
        topk_vals, topk_idx = jax.lax.top_k(probs, TOPK)
        dense_gate = jnp.zeros((N, E), probs.dtype).at[jnp.arange(N)[:, None], topk_idx].set(topk_vals)
        h = jax.nn.relu(jnp.einsum('nd,edh->neh', x_flat, w1) + b1)
        y = jnp.einsum('neh,eho->neo', h, w2) + b2
        out_flat = jnp.einsum('ne,neo->no', dense_gate, y)
        return out_flat.reshape(Bb, Ll, O)
    x = L0_attn_x
    x = x + 0.5 * _L0_ffn_ref(_layernorm(x, axis=-1), L0_ffn_gate_w, L0_ffn_gate_b, L0_ffn_w1, L0_ffn_b1, L0_ffn_w2, L0_ffn_b2)
    x = x + _L0_attn_ref(_layernorm(x, axis=-1), L0_attn_gamma, L0_attn_w_q, L0_attn_w_kv, L0_attn_w_out)
    x = x + 0.5 * _L0_ffn_ref(_layernorm(x, axis=-1), L0_ffn_gate_w, L0_ffn_gate_b, L0_ffn_w1, L0_ffn_b1, L0_ffn_w2, L0_ffn_b2)
    return x

_drawn_inputs = setup_inputs


def setup_inputs(seed=0):
    import zlib

    import numpy as np

    out = dict(_drawn_inputs(seed))
    spreads = {'L0_attn_gamma': (1.0, 0.2),
     'L0_ffn_gate_b': (0.0, 0.8),
     'L0_ffn_b1': (0.0, 0.49),
     'L0_ffn_b2': (0.0, 0.1)}
    factors = {}
    for name, (base, spread) in spreads.items():
        noise = np.random.default_rng([zlib.crc32(name.encode()), seed]).standard_normal(out[name].shape)
        drawn = base * np.exp(spread * noise) if base else spread * noise
        out[name] = jnp.asarray(drawn.astype(out[name].dtype))
    for name, factor in factors.items():
        out[name] = (out[name] * factor).astype(out[name].dtype)
    return out
```

```python
from contextlib import ExitStack

import concourse.bass as bass
from concourse import mybir

F32 = mybir.dt.float32
F32R = mybir.dt.float32r
ALU = mybir.AluOpType
ACT = mybir.ActivationFunctionType
AX_X = mybir.AxisListType.X

P = 128
NB, T, D = 8, 512, 128
TC = T // P
E, H = 8, 512
KC = H // P
CHUNKS = E * KC
UNITS = CHUNKS // 2
LAG = 4
HEADS, DH = 8, 16
VW = DH + 1
STEP = 64
LN_EPS, DEN_EPS, NORM_EPS = 1e-5, 1e-5, 1e-12
FFN1, FFN2 = 0, 1


def ffn_number(stage, j):
    if stage == FFN1:
        return 0 if isinstance(j, int) and j == 0 else j * 2 - 1
    return 2 * NB - 1 if isinstance(j, int) and j == NB - 1 else j * 2 + 2


def need(eng, sem, count):
    if not (isinstance(count, int) and count <= 0):
        eng.wait_ge(sem, count)


def lo_count(f, c):
    return f * (CHUNKS // 2) + c // 2 + 1


def macaron(nc, x_d, gamma_d, wq_d, wkv_d, wo_d, gw_d, gb_d, w1_d, b1_d, w2_d, b2_d, out_d):
    with ExitStack() as ctx:
        def sb(name, shape, dt=F32):
            return ctx.enter_context(nc.sbuf_tensor(name, shape, dt))

        def pb(name, shape):
            return ctx.enter_context(nc.psum_tensor(name, shape, F32))

        def sem(name):
            return ctx.enter_context(nc.semaphore(name))

        w1h, w1l = sb("w1h", [P, E, H], F32R), sb("w1l", [P, E, H], F32R)
        w2h, w2l = sb("w2h", [P, E, KC, D], F32R), sb("w2l", [P, E, KC, D], F32R)
        b1c, b2c = sb("b1c", [P, E * KC]), sb("b2c", [P, E])
        gwf = sb("gwf", [P, E])
        gwh, gwl = sb("gwh", [P, E], F32R), sb("gwl", [P, E], F32R)
        gbb = sb("gbb", [P, E])
        wqk_h, wqk_l = sb("wqk_h", [P, 2, 4, P], F32R), sb("wqk_l", [P, 2, 4, P], F32R)
        wvh, wvl = sb("wvh", [P, D], F32R), sb("wvl", [P, D], F32R)
        woh, wol = sb("woh", [P, D], F32R), sb("wol", [P, D], F32R)
        gam = sb("gam", [P, 1])
        ident = sb("ident", [P, P])
        pick = sb("pick", [2 * E, E, P], F32R)
        rank = sb("rank", [P, TC, E])
        lomask = sb("lomask", [P, 2, 1])
        ones = sb("ones", [P, 2], F32R)
        onef, mhalf, eps = sb("onef", [P, 1]), sb("mhalf", [P, TC]), sb("eps", [P, TC])
        idle = sb("idle", [P, 2])
        x0, x1, x2 = sb("x0", [P, TC, D]), sb("x1", [P, TC, D]), sb("x2", [P, TC, D])
        xn = sb("xn", [P, TC, D])
        stats, mv = sb("stats", [P, TC, 6]), sb("mv", [P, TC, 2])
        rstd, rms = sb("rstd", [P, TC]), sb("rms", [P, TC])
        xTh = [sb(f"xTh{s}", [P, T], F32R) for s in range(2)]
        xTl = [sb(f"xTl{s}", [P, T], F32R) for s in range(2)]
        hf = sb("hf", [P, LAG, T])
        hh = sb("hh", [P, 2 * LAG, T], F32R)
        hl = sb("hl", [P, LAG, T], F32R)
        gate, gy, acc = sb("gate", [P, T]), sb("gy", [P, T]), sb("acc", [P, T])
        lg, pr, pr2, tmp = (sb(n, [P, TC, E]) for n in ("lg", "pr", "pr2", "tmp"))
        f1, f2 = sb("f1", [P, TC, E]), sb("f2", [P, TC, E])
        red, rcp = sb("red", [P, TC]), sb("rcp", [P, TC])
        gcat = [sb(f"gcat{s}", [P, TC, 2 * E]) for s in range(2)]
        gTs = [sb(f"gTs{s}", [2 * E, T], F32R) for s in range(2)]
        nTh, nTl = sb("nTh", [P, T], F32R), sb("nTl", [P, T], F32R)
        qk = sb("qk", [P, 2, 4, T], F32R)
        vp = sb("vp", [P, TC, HEADS * 2 * VW + P - 2 * VW], F32R)
        vps = vp[:, :, 0:HEADS * 2 * VW].rearrange("p c (h v) -> p c h v", v=2 * VW)
        vsum = sb("vsum", [P, HEADS, 2])
        Pf = sb("Pf", [P, 2, 2, T])
        Ph, Pl = sb("Ph", [P, 4, 2, T], F32R), sb("Pl", [P, 2, 2, T], F32R)
        osb = sb("osb", [2 * VW, 2, T])
        nsum, nrec = sb("nsum", [P, 2, TC, VW]), sb("nrec", [P, 2, TC, 1])
        on = sb("on", [P, TC, D])
        onTh, onTl = sb("onTh", [P, T], F32R), sb("onTl", [P, T], F32R)

        z = pb("z", [P, 2, T])
        y = pb("y", [P, T])
        G = pb("G", [P, T])
        S = pb("S", [P, 2, T])
        O = pb("O", [P, T])
        TT = pb("TT", [P, T])

        x_loaded, w_loaded = sem("x_loaded"), [sem(f"w_loaded{k}") for k in range(4)]
        ffn_loaded, attn_loaded, stored = sem("ffn_loaded"), sem("attn_loaded"), sem("stored")
        zeroed, cst, cst_dve = sem("zeroed"), sem("cst"), sem("cst_dve")
        w_hi, w_lo, small_w, small_step = sem("w_hi"), sem("w_lo"), sem("small_w"), sem("small_step")
        z_done, relu_done, h_hi = sem("z_done"), sem("relu_done"), sem("h_hi")
        h_lo = [sem("h_lo_pool"), sem("h_lo_dve")]
        y_part, gbc_full, gy_done, acc_done = sem("y_part"), sem("gbc_full"), sem("gy_done"), sem("acc_done")
        gate_ready = sem("gate_ready")
        accT_full, x1_ready, out_ready = sem("accT_full"), sem("x1_ready"), sem("out_ready")
        rstd_ready, rms_step = [sem(f"rstd_ready{s}") for s in range(3)], [sem(f"rms_step{s}") for s in range(3)]
        rms_done = sem("rms_done")
        ln_step, xn_ready = [sem(f"ln_step{s}") for s in range(3)], [sem(f"xn_ready{s}") for s in range(3)]
        xT_full, xT_hi, xT_lo = ([sem(f"{n}{s}") for s in range(3)] for n in ("xT_full", "xT_hi", "xT_lo"))
        logit_full, shifted, exp_done, gate_step, gates_ready, gT_full, gT_ready = (
            [sem(f"{n}{s}") for s in range(2)] for n in
            ("logit_full", "shifted", "exp_done", "gate_step", "gates_ready", "gT_full", "gT_ready"))
        v_full, v_hi, v_lo, vsum_full, vsum_ready = (
            sem(n) for n in ("v_full", "v_hi", "v_lo", "vsum_full", "vsum_ready"))
        qk_full, qk_hi, qk_ready = sem("qk_full"), sem("qk_hi"), sem("qk_ready")
        s_full, p_hi, p_full, p_lo, pv_done = (sem(n) for n in ("s_full", "p_hi", "p_full", "p_lo", "pv_done"))
        o_ready, oT_full, norm_step, norm_done = (sem(n) for n in ("o_ready", "oT_full", "norm_step", "norm_done"))
        onT_full, onT_hi, onT_lo, proj_full, x2_ready = (
            sem(n) for n in ("onT_full", "onT_hi", "onT_lo", "proj_full", "x2_ready"))

        stage = Pf[:, :, :, :].rearrange("p a b t -> p (a b) t")
        parts = [(w, e) for e in range(E) for w in (1, 2)]
        part_hi = [w1h[:, e, :] if w == 1 else w2h[:, e, :, :].rearrange("p k d -> p (k d)") for w, e in parts]
        part_lo = [w1l[:, e, :] if w == 1 else w2l[:, e, :, :].rearrange("p k d -> p (k d)") for w, e in parts]
        wqkv_s = x1[:, :, :].rearrange("p c d -> p (c d)")[:, 0:3 * D]
        wo_s = x2[:, 0, :]
        NORM_STEPS = 4
        LN_STEPS = 2 * TC
        GATE_A, GATE_B = 9, 10

        def lo_ready(eng, f, c):
            need(eng, h_lo[c % 2], lo_count(f, c))

        block = ctx.enter_context(nc.Block())

        def pipeline(eng, phase_a, phase_b, finish):
            phase_b(0)
            for i in (1,):
                phase_a(i)
                phase_b(i)
            with eng.Fori(2, NB - 1) as i:
                phase_a(i)
                phase_b(i)
            phase_a(NB - 1)
            phase_b(NB - 1)
            phase_a(NB)
            phase_b(NB)
            finish()

        def is_last(i):
            return isinstance(i, int) and i == NB

        @block.sync
        def _(sp):
            def load_x(j):
                if not (isinstance(j, int) and j == 0):
                    need(sp, x1_ready, j)
                sp.dma_start(x0[:, :, :], x_d[j, :, :].rearrange("(p c) d -> p c d", c=TC)).then_inc(x_loaded, 16)

            load_x(0)
            sp.dma_start(gwf[:, :], gw_d).then_inc(ffn_loaded, 16)
            sp.dma_start(gbb[:, :], gb_d.partition_broadcast(P)).then_inc(ffn_loaded, 16)
            sp.dma_start(b1c[:, :], b1_d).then_inc(ffn_loaded, 16)
            sp.dma_start(b2c[:, :], b2_d).then_inc(ffn_loaded, 16)
            for n, (w, e) in enumerate(parts):
                need(sp, w_lo, n - 3)
                if w == 1:
                    sp.dma_start(stage[:, n % 4, :], w1_d[e, :, :]).then_inc(w_loaded[n % 4], 16)
                else:
                    sp.dma_start(stage[:, n % 4, :].rearrange("p (k d) -> p k d", k=KC),
                                 w2_d[e, :, :].rearrange("(k p) d -> p k d", p=P)).then_inc(w_loaded[n % 4], 16)
                if n == 3:
                    sp.dma_start(gam[:, :], gamma_d).then_inc(attn_loaded, 16)
                    sp.dma_start(wqkv_s[:, 0:D], wq_d).then_inc(attn_loaded, 16)
                    sp.dma_start(wqkv_s[:, D:3 * D], wkv_d).then_inc(attn_loaded, 16)
                    sp.dma_start(wo_s, wo_d).then_inc(attn_loaded, 16)

            def store(j):
                sp.wait_ge(out_ready, j + 1)
                sp.dma_start(out_d[j, :, :].rearrange("(p c) d -> p c d", c=TC), x2[:, :, :]).then_inc(stored, 16)

            def phase_a(i):
                if not (isinstance(i, int) and i < 2):
                    store(i - 2)

            def phase_b(i):
                if not (isinstance(i, int) and i > NB - 2):
                    load_x(i + 1)

            pipeline(sp, phase_a, phase_b, lambda: store(NB - 1))
            sp.wait_ge(stored, 16 * NB)

        @block.gpsimd
        def _(pool):
            pool.memset(ident[:, :], 0.0).then_inc(zeroed, 1)
            pool.memset(hf[0:2 * E, 0:2, :], 0.0).then_inc(zeroed, 1)
            pool.memset(ones[:, :].bitcast(F32), 1.0).then_inc(cst, 1)
            pool.memset(onef[:, :], 1.0).then_inc(cst, 1)
            pool.memset(mhalf[:, :], -0.5).then_inc(zeroed, 1)
            pool.memset(eps[:, :], LN_EPS).then_inc(zeroed, 1)
            for e in range(E):
                pool.memset(rank[:, :, e:e + 1], float(E - e)).then_inc(cst, 1)
            pool.memset(vp[:, :, :].bitcast(F32), 0.0).then_inc(zeroed, 1)
            pool.wait_ge(zeroed, 1)
            pool.affine_select(out=ident[:, :], in_=ident[:, :], compare_op=ALU.not_equal, fill=1.0, base=0,
                               pattern=[[-1, P]], channel_multiplier=1).then_inc(cst, 1)
            pool.wait_ge(zeroed, 2)
            pk = hf[0:2 * E, 0:2, :].rearrange("k a t -> k (a t)").rearrange("k (e p) -> k e p", e=E)
            pool.affine_select(out=pk, in_=pk, compare_op=ALU.not_equal, fill=1.0, base=0,
                               pattern=[[-1, E], [0, P]], channel_multiplier=1).then_inc(zeroed, 1)
            pool.wait_ge(zeroed, 6)
            pool.affine_select(out=pk, in_=pk, compare_op=ALU.not_equal, fill=1.0, base=-E,
                               pattern=[[-1, E], [0, P]], channel_multiplier=1).then_inc(cst, 1)
            pool.wait_ge(zeroed, 5)
            pool.memset(vps[:, :, :, DH:VW].bitcast(F32), 1.0).then_inc(cst, 1)

            def split_h(f, c):
                pool.wait_ge(h_hi, f * CHUNKS + c + 1)
                need(pool, y_part, f * CHUNKS + c - LAG + 1)
                pool.tensor_tensor(hl[:, c % LAG, :], hf[:, c % LAG, :], hh[:, c % (2 * LAG), :].bitcast(F32),
                                   ALU.subtract).then_inc(h_lo[0], 1)

            def add_gated(f, e):
                pool.wait_ge(gy_done, f * 8 + e + 1)
                need(pool, acc_done, f * 7 + e - 1)
                pool.tensor_tensor(acc[:, :], acc[:, :], gy[:, :], ALU.add).then_inc(acc_done, 1)

            def inverse_deviation(s, j):
                pool.wait_ge(ln_step[s], (j + 1) * LN_STEPS)
                step = rms_step[s]
                n = j * (5 if s == 2 else 1)
                pool.tensor_tensor(rstd[:, :], mv[:, :, 1], eps[:, :], ALU.add).then_inc(step, 1)
                pool.wait_ge(step, n + 1)
                last = pool.tensor_tensor(rstd[:, :], rstd[:, :], mhalf[:, :], ALU.pow)
                if s == 2:
                    last.then_inc(step, 1)
                    pool.wait_ge(step, n + 2)
                    pool.tensor_tensor(rms[:, :], mv[:, :, 1], rstd[:, :], ALU.mult).then_inc(step, 1)
                    pool.wait_ge(step, n + 3)
                    pool.tensor_tensor(rms[:, :], rms[:, :], rstd[:, :], ALU.mult).then_inc(step, 1)
                    pool.wait_ge(step, n + 4)
                    pool.tensor_tensor(idle[:, 0:1], eps[:, 0:1], eps[:, 0:1], ALU.add)
                    pool.tensor_scalar(rms[:, :], rms[:, :], NORM_EPS ** 2 / D, None, ALU.max).then_inc(step, 1)
                    pool.wait_ge(step, n + 5)
                    pool.tensor_tensor(rms[:, :], rms[:, :], mhalf[:, :], ALU.pow).then_inc(rms_done, 1)
                    pool.wait_ge(rms_done, j + 1)
                    last = pool.tensor_tensor(rstd[:, :], rms[:, :], rstd[:, :], ALU.mult)
                last.then_inc(rstd_ready[s], 1)

            def slots(f, before, norms):
                for u in range(UNITS):
                    if u in norms:
                        inverse_deviation(*norms[u])
                    if before is not None and u in (0, 2):
                        add_gated(before, 6 + u // 2)
                    if f is not None:
                        if u >= 6 and u % 2 == 0:
                            add_gated(f, u // 2 - 2)
                        split_h(f, 2 * u)

            def phase_a(i):
                f = None if is_last(i) else ffn_number(FFN1, i)
                slots(f, None if isinstance(i, int) and i < 2 else ffn_number(FFN2, i - 2), {12: (FFN2, i - 1)})

            def phase_b(i):
                f = None if isinstance(i, int) and i == 0 else ffn_number(FFN2, i - 1)
                norms = {} if is_last(i) else {5: (2, i)}
                if not (isinstance(i, int) and i >= NB - 1):
                    norms[8] = (FFN1, i + 1)
                slots(f, None if is_last(i) else ffn_number(FFN1, i), norms)

            inverse_deviation(FFN1, 0)
            slots(0, None, {})
            pipeline(pool, phase_a, phase_b, lambda: slots(None, ffn_number(FFN2, NB - 1), {}))

        @block.scalar
        def _(act):
            def relu(f, u, cc):
                c = 2 * u + cc
                act.wait_ge(z_done, f * 32 + c + 1)
                lo_ready(act, f, c - LAG)
                act.activation(hf[:, c % LAG, :], z[:, c % 2, :], ACT.Relu,
                               bias=b1c[:, c:c + 1]).then_inc(relu_done, 1)

            def copy_gate(f, e):
                act.wait_ge(gbc_full, f * 8 + e + 1)
                need(act, gy_done, f * 8 + e)
                act.activation(gate[:, :], G[:, :], ACT.Copy).then_inc(gate_ready, 1)

            def squares(j, p):
                act.wait_ge(s_full, j * 16 + p + 1)
                need(act, pv_done, j * 16 + p - 3)
                act.activation(Ph[:, p % 4, :, :], S[:, :, :], ACT.Square, bias=onef[:, :]).then_inc(p_hi, 1)
                need(act, p_lo, j * 16 + p - 1)
                if p < 2:
                    need(act, qk_ready, j * 8 + 8)
                act.activation(Pf[:, p % 2, :, :], S[:, :, :], ACT.Square, bias=onef[:, :]).then_inc(p_full, 1)

            def head_out(j, h):
                act.wait_ge(pv_done, j * 16 + 2 * h + 2)
                if h == 0:
                    act.wait_ge(vsum_ready, j + 1)
                need(act, oT_full, j * 8 + h - 1)
                act.activation(osb[:, h % 2, :], O[0:2 * VW, :], ACT.Identity,
                               bias=vsum[0:2 * VW, h, 0:1]).then_inc(o_ready, 1)

            def round_xT(s, j, bank):
                act.wait_ge(xT_full[s], j + 1)
                if s == 2:
                    need(act, qk_full, j * 8)
                elif not (isinstance(j, int) and j == 0):
                    act.wait_ge(z_done, ffn_number(s, j - 1) * 32 + 32)
                dst = nTh if s == 2 else xTh[s]
                act.activation(dst[:, :], bank, ACT.Copy).then_inc(xT_hi[s], 1)

            def exps(s, j):
                act.wait_ge(shifted[s], j + 1)
                act.activation(tmp[:, :, :], lg[:, :, :], ACT.Exp).then_inc(exp_done[s], 1)

            def copy_gT(s, j, bank):
                act.wait_ge(gT_full[s], j + 1)
                if not (isinstance(j, int) and j == 0):
                    act.wait_ge(gbc_full, ffn_number(s, j - 1) * 8 + 8)
                act.activation(gTs[s][:, :], bank[0:2 * E, :], ACT.Copy).then_inc(gT_ready[s], 1)

            def slots(f, heads, before, misc):
                for u in range(UNITS):
                    if heads is not None and u < 8:
                        squares(heads, 2 * u)
                    if f is not None:
                        relu(f, u, 0)
                    if heads is not None and u < 8:
                        squares(heads, 2 * u + 1)
                    if f is not None:
                        relu(f, u, 1)
                    if heads is not None and 1 <= u <= 8:
                        head_out(heads, u - 1)
                    if before is not None and u == 1:
                        copy_gate(before, 7)
                    if f is not None and u == 2:
                        copy_gate(f, 0)
                    if f is not None and u >= 5 and u % 2 == 1:
                        copy_gate(f, (u - 3) // 2)
                    misc(u)

            def phase_a(i):
                def misc(u):
                    j = i - 1
                    if u == 10:
                        act.wait_ge(onT_full, j + 1)
                        need(act, proj_full, j)
                        act.activation(onTh[:, :], S[:, 0, :], ACT.Copy).then_inc(onT_hi, 1)
                    if u == 13:
                        round_xT(FFN2, j, S[:, 0, :])
                    if u == 14:
                        exps(FFN2, j)
                slots(None if is_last(i) else ffn_number(FFN1, i), i - 1,
                      None if isinstance(i, int) and i < 2 else ffn_number(FFN2, i - 2), misc)

            def phase_b(i):
                def misc(u):
                    if u == 0 and not (isinstance(i, int) and i == 0):
                        copy_gT(FFN2, i - 1, S[:, 1, :])
                    if is_last(i):
                        return
                    if u == 6:
                        round_xT(2, i, O[:, :])
                    if u == 7:
                        act.wait_ge(v_full, i + 1)
                        need(act, pv_done, i * 16)
                        act.activation(vps[:, :, :, 0:DH], TT[:, :].rearrange("p (c h e) -> p c h e", c=TC, h=HEADS),
                                       ACT.Copy).then_inc(v_hi, 1)
                    if u == 8:
                        act.wait_ge(vsum_full, i + 1)
                        need(act, o_ready, i * 8)
                        act.activation(vsum[:, :, :], TT[:, 0:2 * HEADS].rearrange("p (h a) -> p h a", a=2),
                                       ACT.Copy).then_inc(vsum_ready, 1)
                    if 8 <= u < 12:
                        for t in range(2 * (u - 8), 2 * (u - 8) + 2):
                            act.wait_ge(qk_full, i * 8 + t + 1)
                            if t >= 2:
                                act.wait_ge(qk_ready, i * 8 + t - 1)
                            else:
                                need(act, p_lo, i * 16)
                            act.activation(Pf[:, t % 2, 0, :].bitcast(F32R), S[:, t % 2, :],
                                           ACT.Copy).then_inc(qk_hi, 1)
                    if isinstance(i, int) and i == NB - 1:
                        return
                    if u == 9:
                        round_xT(FFN1, i + 1, O[:, :])
                    if u == 10:
                        exps(FFN1, i + 1)
                    if u == 12:
                        copy_gT(FFN1, i + 1, O[:, :])
                first = isinstance(i, int) and i == 0
                slots(None if first else ffn_number(FFN2, i - 1), None,
                      None if is_last(i) else ffn_number(FFN1, i), misc)

            def round_part(n):
                act.wait_ge(w_loaded[n % 4], 16 * (n // 4 + 1))
                act.activation(part_hi[n], stage[:, n % 4, :], ACT.Copy).then_inc(w_hi, 1)

            for n in range(4):
                round_part(n)
                if n == 0:
                    round_xT(FFN1, 0, O[:, :])
                if n == 1:
                    exps(FFN1, 0)
                if n == 2:
                    copy_gT(FFN1, 0, O[:, :])
                    act.wait_ge(cst, 2)
            act.wait_ge(cst_dve, 1)
            act.wait_ge(ffn_loaded, 16 * 4)
            slots(0, None, None, lambda u: round_part(u + 4) if u + 4 < len(parts) else None)
            act.wait_ge(w_lo, len(parts))
            pipeline(act, phase_a, phase_b, lambda: copy_gate(ffn_number(FFN2, NB - 1), 7))

        @block.tensor
        def _(pe):
            def three(out, a_hi, a_lo, b_hi, b_lo, start, stop):
                pe.matmul(out, a_hi, b_hi, start=start, stop=False)
                pe.matmul(out, a_hi, b_lo, start=False, stop=False)
                return pe.matmul(out, a_lo, b_hi, start=False, stop=stop)

            def mm1(s, f, u, cc):
                c = 2 * u + cc
                k = c % KC
                if isinstance(f, int) and f == 0 and cc == 0 and u % 2 == 0:
                    pe.wait_ge(w_lo, u + 1)
                need(pe, relu_done, f * 32 + c - 1)
                w = slice(k * P, k * P + P)
                three(z[:, c % 2, :], w1h[:, u // 2, w], w1l[:, u // 2, w], xTh[s][:, :], xTl[s][:, :],
                      True, True).then_inc(z_done, 1)

            def mm2(f, c):
                e, k = c // KC, c % KC
                if isinstance(f, int) and f == 0 and k == 0:
                    pe.wait_ge(w_lo, 2 * e + 2)
                lo_ready(pe, f, c)
                if k == 0:
                    need(pe, gy_done, f * 8 + e)
                three(y[:, :], w2h[:, e, k, :], w2l[:, e, k, :], hh[:, c % (2 * LAG), :], hl[:, c % LAG, :],
                      k == 0, k == KC - 1).then_inc(y_part, 1)

            def spread_gate(s, j, f, e):
                if e == 0:
                    pe.wait_ge(gT_ready[s], j + 1)
                need(pe, gate_ready, f * 8 + e)
                if e == 1:
                    if s == FFN1 or isinstance(j, int) and j == NB - 1:
                        need(pe, out_ready, j - 1 if s == FFN1 else j)
                    else:
                        pe.wait_ge(x1_ready, j + 2)
                pe.matmul(G[:, :], pick[:, e, :], gTs[s][:, :], start=True, stop=True).then_inc(gbc_full, 1)

            def transpose_sum(f, gates):
                pe.wait_ge(acc_done, f * 7 + 7)
                pe.wait_ge(gate_ready, gates)
                for c in range(TC):
                    mm = pe.transpose(G[:, c * P:c * P + P], acc[:, c * P:c * P + P], ident[:, :])
                mm.then_inc(accT_full, 1)

            def scores(j, p):
                h = p // 2
                if p == 0:
                    pe.wait_ge(qk_ready, j * 8 + 8)
                need(pe, p_full, j * 16 + p)
                rows = slice(STEP * (h % 2), STEP * (h % 2) + STEP)
                for mc in range(2):
                    m = 2 * (p % 2) + mc
                    mm = pe.matmul(S[:, mc, :], qk[rows, 1, h // 2, m * P:m * P + P], qk[rows, 0, h // 2, :],
                                   start=True, stop=True)
                mm.then_inc(s_full, 1)

            def weigh(j, p):
                h = p // 2
                pe.wait_ge(p_lo, j * 16 + p + 1)
                if p % 2 == 0:
                    need(pe, o_ready, j * 8 + h)
                for mc in range(2):
                    m = 2 * (p % 2) + mc
                    v = vp[:, m, h * 2 * VW:h * 2 * VW + P]
                    pe.matmul(O[:, :], v, Ph[:, p % 4, mc, :], start=(m == 0), stop=False)
                    mm = pe.matmul(O[:, :], v, Pl[:, p % 2, mc, :], start=False, stop=(m == TC - 1))
                mm.then_inc(pv_done, 1)

            def transpose_head(j, h):
                pe.wait_ge(o_ready, j * 8 + h + 1)
                if h % 2 == 0:
                    need(pe, norm_done, j * 4 + h // 2)
                at = (h % 2) * TC * 2 * VW
                pe.matmul(TT[:, at:at + 1], ident[:, :], ident[:, 0:1], start=True, stop=True)
                for c in range(TC):
                    at = ((h % 2) * TC + c) * 2 * VW
                    mm = pe.transpose(TT[:, at:at + 2 * VW], osb[:, h % 2, c * P:c * P + P], ident[0:2 * VW, 0:2 * VW])
                mm.then_inc(oT_full, 1)

            def transpose_xn(s, j, bank):
                pe.wait_ge(xn_ready[s], j + 1)
                for c in range(TC):
                    mm = pe.transpose(bank[:, c * P:c * P + P], xn[:, c, :], ident[:, :])
                mm.then_inc(xT_full[s], 1)

            def logits(s, j):
                pe.wait_ge(xT_hi[s], j + 1)
                pe.wait_ge(xT_lo[s], j + 1)
                for c in range(TC):
                    tok = slice(c * P, c * P + P)
                    mm = three(TT[:, c * E:c * E + E], xTh[s][:, tok], xTl[s][:, tok], gwh[:, :], gwl[:, :], True, True)
                mm.then_inc(logit_full[s], 1)

            def transpose_gates(s, j, bank):
                pe.wait_ge(gates_ready[s], j + 1)
                for c in range(TC):
                    mm = pe.transpose(bank[0:2 * E, c * P:c * P + P], gcat[s][:, c, :], ident[:, :])
                mm.then_inc(gT_full[s], 1)

            def slots(s, j, f, heads, before, misc):
                for u in range(UNITS):
                    if heads is not None and u < 8:
                        scores(heads, 2 * u)
                    def second(cc):
                        c = 2 * u + cc - LAG
                        if c < 0:
                            if before is not None:
                                mm2(before, CHUNKS + c)
                        elif f is not None:
                            mm2(f, c)

                    late = u % 2 == 0
                    if f is not None:
                        mm1(s, f, u, 0)
                    if not late:
                        second(0)
                    if heads is not None and 1 <= u <= 8:
                        weigh(heads, 2 * u - 2)
                    if heads is not None and u < 8:
                        scores(heads, 2 * u + 1)
                    if f is not None:
                        mm1(s, f, u, 1)
                    if late:
                        second(0)
                    second(1)
                    if heads is not None and 1 <= u <= 8:
                        weigh(heads, 2 * u - 1)
                    if u == 0 and before is not None:
                        spread_gate(1 - s, before_tile[0], before, 7)
                    if u == 1 and f is not None:
                        spread_gate(s, j, f, 0)
                    if u == 3 and before is not None:
                        transpose_sum(before, before * 8 + (8 if f is None else 9))
                    if u >= 4 and u % 2 == 0 and f is not None:
                        spread_gate(s, j, f, (u - 2) // 2)
                    if heads is not None and 2 <= u <= 9:
                        transpose_head(heads, u - 2)
                    misc(u)

            before_tile = [None]

            def phase_a(i):
                first = isinstance(i, int) and i < 2
                before_tile[0] = None if first else i - 2

                def misc(u):
                    j = i - 1
                    if u == 10:
                        pe.wait_ge(norm_done, j * 4 + 4)
                        pe.wait_ge(p_full, j * 16 + 16)
                        for c in range(TC):
                            mm = pe.transpose(S[:, 0, c * P:c * P + P], on[:, c, :], ident[:, :])
                        mm.then_inc(onT_full, 1)
                    if u == 11:
                        pe.wait_ge(onT_hi, j + 1)
                        pe.wait_ge(onT_lo, j + 1)
                        for c in range(TC):
                            tok = slice(c * P, c * P + P)
                            mm = three(O[:, tok], onTh[:, tok], onTl[:, tok], woh[:, :], wol[:, :], True, True)
                        mm.then_inc(proj_full, 1)
                    if u == 13:
                        transpose_xn(FFN2, j, S[:, 0, :])
                    if u == 14:
                        logits(FFN2, j)

                slots(FFN1, i, None if is_last(i) else ffn_number(FFN1, i), i - 1,
                      None if first else ffn_number(FFN2, i - 2), misc)

            def phase_b(i):
                before_tile[0] = i

                def misc(u):
                    if u == 0 and not (isinstance(i, int) and i == 0):
                        transpose_gates(FFN2, i - 1, S[:, 1, :])
                    if is_last(i):
                        return
                    if u == 6:
                        need(pe, x2_ready, i)
                        transpose_xn(2, i, O[:, :])
                    if u == 7:
                        pe.wait_ge(xT_hi[2], i + 1)
                        pe.wait_ge(xT_lo[2], i + 1)
                        need(pe, shifted[FFN2], i)
                        for c in range(TC):
                            tok = slice(c * P, c * P + P)
                            mm = three(TT[:, tok], nTh[:, tok], nTl[:, tok], wvh[:, :], wvl[:, :], True, True)
                        mm.then_inc(v_full, 1)
                    if u == 8:
                        pe.wait_ge(v_hi, i + 1)
                        pe.wait_ge(v_lo, i + 1)
                        for h in range(HEADS):
                            for c in range(TC):
                                mm = pe.matmul(TT[:, 2 * h:2 * h + 2], vp[:, c, h * 2 * VW:h * 2 * VW + P], ones[:, :],
                                               start=(c == 0), stop=(c == TC - 1))
                        mm.then_inc(vsum_full, 1)
                        need(pe, gT_ready[FFN2], i)
                    if 8 <= u < 12:
                        for t in range(2 * (u - 8), 2 * (u - 8) + 2):
                            if t >= 2:
                                pe.wait_ge(qk_ready, i * 8 + t - 1)
                            three(S[:, t % 2, :], wqk_h[:, t % 2, t // 2, :], wqk_l[:, t % 2, t // 2, :],
                                  nTh[:, :], nTl[:, :], True, True).then_inc(qk_full, 1)
                    if isinstance(i, int) and i == NB - 1:
                        return
                    if u == 9:
                        transpose_xn(FFN1, i + 1, O[:, :])
                    if u == 10:
                        pe.wait_ge(vsum_ready, i + 1)
                        logits(FFN1, i + 1)
                    if u == 12:
                        transpose_gates(FFN1, i + 1, O[:, :])

                first = isinstance(i, int) and i == 0
                slots(FFN2, i - 1, None if first else ffn_number(FFN2, i - 1), None,
                      None if is_last(i) else ffn_number(FFN1, i), misc)

            def finish():
                f = ffn_number(FFN2, NB - 1)
                for u in range(2):
                    for cc in range(2):
                        mm2(f, CHUNKS - LAG + 2 * u + cc)
                    if u == 0:
                        spread_gate(FFN2, NB - 1, f, 7)
                transpose_sum(f, f * 8 + 8)

            pe.wait_ge(cst, 11)
            transpose_xn(FFN1, 0, O[:, :])
            pe.wait_ge(small_w, 2)
            logits(FFN1, 0)
            transpose_gates(FFN1, 0, O[:, :])
            pe.wait_ge(cst_dve, 1)
            slots(FFN1, 0, 0, None, None, lambda u: None)
            pe.wait_ge(small_w, 10)
            pipeline(pe, phase_a, phase_b, finish)

        @block.vector
        def _(dve):
            def bc(ap, n):
                return ap.unsqueeze(2).to_broadcast([P, TC, n])

            def split_h(f, c):
                dve.wait_ge(relu_done, f * CHUNKS + c + 1)
                need(dve, y_part, f * CHUNKS + c - 2 * LAG + 1)
                dve.tensor_copy(hh[:, c % (2 * LAG), :], hf[:, c % LAG, :]).then_inc(h_hi, 1)
                if c % 2 == 1:
                    dve.wait_ge(h_hi, f * CHUNKS + c + 1)
                    need(dve, y_part, f * CHUNKS + c - LAG + 1)
                    dve.tensor_tensor(hl[:, c % LAG, :], hf[:, c % LAG, :], hh[:, c % (2 * LAG), :].bitcast(F32),
                                      ALU.subtract).then_inc(h_lo[1], 1)

            def gate_y(f, e):
                dve.wait_ge(y_part, f * CHUNKS + KC * (e + 1))
                dve.wait_ge(gate_ready, f * 8 + e + 1)
                if e == 0:
                    need(dve, accT_full, f)
                else:
                    need(dve, acc_done, f * 7 + e - 1)
                dve.scalar_tensor_tensor(acc[:, :] if e == 0 else gy[:, :], y[:, :], b2c[:, e:e + 1], gate[:, :],
                                         ALU.add, ALU.mult).then_inc(gy_done, 1)

            def split_p(j, p):
                dve.wait_ge(p_full, j * 16 + p + 1)
                need(dve, pv_done, j * 16 + p - 1)
                dve.tensor_tensor(Pl[:, p % 2, :, :], Pf[:, p % 2, :, :], Ph[:, p % 4, :, :].bitcast(F32),
                                  ALU.subtract).then_inc(p_lo, 1)

            def statistics(s, j, src):
                for c in range(TC):
                    dve.bn_stats(stats[:, c, :], src[:, c, :]).then_inc(ln_step[s], 1)
                dve.wait_ge(ln_step[s], j * LN_STEPS + TC)
                dve.memset(idle[:, 1:2], 0.0)
                for c in range(TC):
                    dve.bn_aggr(mv[:, c, :], stats[:, c, :]).then_inc(ln_step[s], 1)

            def layer_norm(s, j, src):
                dve.wait_ge(rstd_ready[s], j + 1)
                if s == FFN1:
                    need(dve, xT_full[2], j)
                elif s == 2:
                    need(dve, xT_full[FFN2], j)
                    need(dve, xT_full[FFN1], j + 1)
                else:
                    need(dve, xT_full[FFN1], j + 2 if not (isinstance(j, int) and j == NB - 1) else NB)
                    need(dve, xT_full[2], j + 1)
                for c in range(TC):
                    ins = dve.tensor_scalar(xn[:, c, :], src[:, c, :], mv[:, c, 0:1], rstd[:, c:c + 1],
                                            ALU.subtract, ALU.mult)
                ins.then_inc(xn_ready[s], 1)

            def split_xT(s, j, bank):
                dve.wait_ge(xT_hi[s], j + 1)
                hi, lo = (nTh, nTl) if s == 2 else (xTh[s], xTl[s])
                dve.tensor_tensor(lo[:, :], bank, hi[:, :].bitcast(F32), ALU.subtract).then_inc(xT_lo[s], 1)

            def shift_logits(s, j):
                n = j * (GATE_A + GATE_B)
                dve.wait_ge(logit_full[s], j + 1)
                dve.tensor_tensor(pr2[:, :, :], TT[:, 0:TC * E].rearrange("p (c e) -> p c e", e=E),
                                  gbb[:, :].unsqueeze(1).to_broadcast([P, TC, E]), ALU.add).then_inc(gate_step[s], 1)
                dve.wait_ge(gate_step[s], n + 1)
                dve.tensor_reduce(red[:, :], pr2[:, :, :], AX_X, ALU.max).then_inc(gate_step[s], 1)
                dve.wait_ge(gate_step[s], n + 2)
                dve.tensor_tensor(lg[:, :, :], pr2[:, :, :], bc(red[:, :], E), ALU.subtract).then_inc(shifted[s], 1)

            def choose(s, n, values, out):
                dve.tensor_reduce(red[:, :], values[:, :, :], AX_X, ALU.max).then_inc(gate_step[s], 1)
                dve.wait_ge(gate_step[s], n + 1)
                dve.tensor_tensor(f2[:, :, :], values[:, :, :], bc(red[:, :], E), ALU.is_equal).then_inc(gate_step[s], 1)
                dve.wait_ge(gate_step[s], n + 2)
                dve.tensor_tensor(lg[:, :, :], f2[:, :, :], rank[:, :, :], ALU.mult).then_inc(gate_step[s], 1)
                dve.wait_ge(gate_step[s], n + 3)
                dve.tensor_reduce(red[:, :], lg[:, :, :], AX_X, ALU.max).then_inc(gate_step[s], 1)
                dve.wait_ge(gate_step[s], n + 4)
                dve.tensor_tensor(out[:, :, :], rank[:, :, :], bc(red[:, :], E), ALU.is_equal).then_inc(gate_step[s], 1)
                dve.wait_ge(gate_step[s], n + 5)

            def probabilities(s, j):
                n = j * (GATE_A + GATE_B) + 2
                dve.wait_ge(exp_done[s], j + 1)
                dve.tensor_reduce(red[:, :], tmp[:, :, :], AX_X, ALU.add).then_inc(gate_step[s], 1)
                dve.wait_ge(gate_step[s], n + 1)
                dve.reciprocal(rcp[:, :], red[:, :]).then_inc(gate_step[s], 1)
                dve.wait_ge(gate_step[s], n + 2)
                dve.tensor_tensor(pr[:, :, :], tmp[:, :, :], bc(rcp[:, :], E), ALU.mult).then_inc(gate_step[s], 1)
                dve.wait_ge(gate_step[s], n + 3)
                choose(s, n + 3, pr, f1)

            def top_two(s, j):
                n = j * (GATE_A + GATE_B) + 10
                dve.scalar_tensor_tensor(pr2[:, :, :], f1[:, :, :], -2.0, pr[:, :, :],
                                         ALU.mult, ALU.add).then_inc(gate_step[s], 1)
                dve.wait_ge(gate_step[s], n + 1)
                choose(s, n + 1, pr2, tmp)
                dve.tensor_tensor(f1[:, :, :], f1[:, :, :], tmp[:, :, :], ALU.add).then_inc(gate_step[s], 1)
                dve.wait_ge(gate_step[s], n + 7)
                dve.tensor_tensor(pr[:, :, :], pr[:, :, :], f1[:, :, :], ALU.mult).then_inc(gate_step[s], 1)
                dve.wait_ge(gate_step[s], n + 8)
                need(dve, gT_full[s], j)
                dve.tensor_copy(gcat[s][:, :, 0:E].bitcast(F32R), pr[:, :, :]).then_inc(gate_step[s], 1)
                dve.wait_ge(gate_step[s], n + 9)
                dve.tensor_tensor(gcat[s][:, :, E:2 * E].bitcast(F32R), pr[:, :, :], gcat[s][:, :, 0:E],
                                  ALU.subtract).then_inc(gates_ready[s], 1)

            def normalise(j, hp):
                n = (j * 4 + hp) * NORM_STEPS
                both = TT[:, 0:4 * TC * VW].rearrange("p (h c v) -> p h c v", h=2, v=2 * VW)
                dve.wait_ge(oT_full, j * 8 + 2 * hp + 2)
                dve.tensor_copy(nsum[:, :, :, :], both[:, :, :, 0:VW]).then_inc(norm_step, 1)
                dve.wait_ge(norm_step, n + 1)
                dve.tensor_tensor(nsum[:, :, :, :], nsum[:, :, :, :], both[:, :, :, VW:2 * VW],
                                  ALU.add).then_inc(norm_step, 1)
                dve.wait_ge(norm_step, n + 2)
                dve.tensor_scalar(nrec[:, :, :, :], nsum[:, :, :, DH:VW], 2 * DEN_EPS, None,
                                  ALU.max).then_inc(norm_step, 1)
                dve.wait_ge(norm_step, n + 3)
                dve.reciprocal(nrec[:, :, :, :], nrec[:, :, :, :]).then_inc(norm_step, 1)
                dve.wait_ge(norm_step, n + 4)
                if hp == 0:
                    need(dve, onT_full, j)
                ins = None
                for h in range(2):
                    head = 2 * hp + h
                    ins = dve.tensor_tensor(on[:, :, head * DH:head * DH + DH], nsum[:, h, :, 0:DH],
                                            nrec[:, h, :, :].to_broadcast([P, TC, DH]), ALU.mult)
                ins.then_inc(norm_done, 1)

            def slots(f, heads, before, misc, residual):
                for u in range(UNITS):
                    if u in (0, 2) and before is not None:
                        gate_y(before, 6 + u // 2)
                    if u >= 4 and u % 2 == 0 and f is not None:
                        gate_y(f, u // 2 - 2)
                    if u > 0 and f is not None:
                        split_h(f, 2 * u - 1)
                    if u == 0 and before is not None:
                        split_h(before, CHUNKS - 1)
                    if u == 4 and before is not None:
                        residual()
                    if heads is not None and u < 8:
                        split_p(heads, 2 * u)
                    if f is not None:
                        split_h(f, 2 * u)
                    if heads is not None and u < 8:
                        split_p(heads, 2 * u + 1)
                    if heads is not None and u in (3, 5, 7, 9):
                        normalise(heads, (u - 3) // 2)
                    misc(u)

            def add_ffn2(j):
                dve.wait_ge(accT_full, ffn_number(FFN2, j) + 1)
                dve.scalar_tensor_tensor(x2[:, :, :], G[:, :].rearrange("p (c d) -> p c d", c=TC), 0.5, x2[:, :, :],
                                         ALU.mult, ALU.add).then_inc(out_ready, 1)

            def phase_a(i):
                def misc(u):
                    j = i - 1
                    if u == 10:
                        dve.wait_ge(onT_hi, j + 1)
                        dve.tensor_tensor(onTl[:, :], S[:, 0, :], onTh[:, :].bitcast(F32),
                                          ALU.subtract).then_inc(onT_lo, 1)
                    if u == 11:
                        dve.wait_ge(proj_full, j + 1)
                        if not (isinstance(i, int) and i < 2):
                            dve.wait_ge(stored, (i - 1) * 16)
                        dve.tensor_tensor(x2[:, :, :], O[:, :].rearrange("p (c d) -> p c d", c=TC), x1[:, :, :],
                                          ALU.add).then_inc(x2_ready, 1)
                        dve.wait_ge(x2_ready, j + 1)
                        statistics(FFN2, j, x2)
                    if u == 12:
                        layer_norm(FFN2, j, x2)
                    if u == 13:
                        split_xT(FFN2, j, S[:, 0, :])
                    if u == 14:
                        shift_logits(FFN2, j)
                    if u == 15:
                        probabilities(FFN2, j)
                        top_two(FFN2, j)

                slots(None if is_last(i) else ffn_number(FFN1, i), i - 1,
                      None if isinstance(i, int) and i < 2 else ffn_number(FFN2, i - 2),
                      misc, lambda: add_ffn2(i - 2))

            def phase_b(i):
                def residual():
                    dve.wait_ge(accT_full, ffn_number(FFN1, i) + 1)
                    dve.scalar_tensor_tensor(x1[:, :, :], G[:, :].rearrange("p (c d) -> p c d", c=TC), 0.5, x0[:, :, :],
                                             ALU.mult, ALU.add).then_inc(x1_ready, 1)

                def misc(u):
                    if is_last(i):
                        return
                    if u == 4:
                        dve.wait_ge(x1_ready, i + 1)
                        statistics(2, i, x1)
                    if u == 5:
                        layer_norm(2, i, x1)
                    if u == 6:
                        split_xT(2, i, O[:, :])
                    if u == 7:
                        dve.wait_ge(v_hi, i + 1)
                        dve.tensor_tensor(vps[:, :, :, VW:VW + DH],
                                          TT[:, :].rearrange("p (c h e) -> p c h e", c=TC, h=HEADS),
                                          vps[:, :, :, 0:DH].bitcast(F32), ALU.subtract).then_inc(v_lo, 1)
                    if 8 <= u < 12:
                        for t in range(2 * (u - 8), 2 * (u - 8) + 2):
                            dve.wait_ge(qk_hi, i * 8 + t + 1)
                            if t == 0:
                                need(dve, s_full, i * 16)
                            dve.scalar_tensor_tensor(qk[:, t % 2, t // 2, :], Pf[:, t % 2, 0, :],
                                                     lomask[:, t % 2, :], S[:, t % 2, :],
                                                     ALU.mult, ALU.add).then_inc(qk_ready, 1)
                    if isinstance(i, int) and i == NB - 1:
                        return
                    if u == 7:
                        dve.wait_ge(x_loaded, (i + 2) * 16)
                        statistics(FFN1, i + 1, x0)
                    if u == 8:
                        layer_norm(FFN1, i + 1, x0)
                    if u == 9:
                        split_xT(FFN1, i + 1, O[:, :])
                    if u == 10:
                        shift_logits(FFN1, i + 1)
                    if u == 11:
                        probabilities(FFN1, i + 1)
                        top_two(FFN1, i + 1)

                first = isinstance(i, int) and i == 0
                slots(None if first else ffn_number(FFN2, i - 1), None,
                      None if is_last(i) else ffn_number(FFN1, i), misc, residual)

            def split_part(n):
                dve.wait_ge(w_hi, n + 1)
                dve.tensor_tensor(part_lo[n], stage[:, n % 4, :], part_hi[n].bitcast(F32),
                                  ALU.subtract).then_inc(w_lo, 1)

            dve.wait_ge(x_loaded, 16)
            statistics(FFN1, 0, x0)
            layer_norm(FFN1, 0, x0)
            dve.wait_ge(ffn_loaded, 16 * 4)
            dve.tensor_copy(gwh[:, :], gwf[:, :]).then_inc(small_w, 1)
            dve.wait_ge(small_w, 1)
            dve.tensor_tensor(gwl[:, :], gwf[:, :], gwh[:, :].bitcast(F32), ALU.subtract).then_inc(small_w, 1)
            split_part(0)
            split_xT(FFN1, 0, O[:, :])
            split_part(1)
            dve.wait_ge(cst, 13)
            shift_logits(FFN1, 0)
            dve.tensor_copy(pick[:, :, :], hf[0:2 * E, 0:2, :].rearrange("k a t -> k (a t)")
                            .rearrange("k (e p) -> k e p", e=E)).then_inc(cst_dve, 1)
            probabilities(FFN1, 0)
            top_two(FFN1, 0)
            for k in range(2):
                first = DH * (1 + k)
                cols = ident[:, :].rearrange("p (g r) -> p g r", r=STEP)[:, :, first:first + DH]
                dve.tensor_reduce(lomask[:, k, :], cols, mybir.AxisListType.XY, ALU.add, negate=True).then_inc(cst_dve, 1)
            split_part(2)
            split_part(3)

            def attention_weights():
                dve.wait_ge(attn_loaded, 16 * 4)
                dve.tensor_scalar(wqkv_s, wqkv_s, gam[:, 0:1], None, ALU.mult).then_inc(small_step, 1)
                dve.memset(wqk_h[:, :, :, :].bitcast(F32), 0.0).then_inc(small_step, 1)
                dve.memset(wqk_l[:, :, :, :].bitcast(F32), 0.0).then_inc(small_step, 1)
                dve.wait_ge(small_step, 3)
                dve.tensor_scalar(wqkv_s[:, 0:D], wqkv_s[:, 0:D], float(DH) ** -0.5, None, ALU.mult).then_inc(small_step, 1)
                dve.wait_ge(small_step, 4)
                for k in range(2):
                    src = wqkv_s[:, k * D:k * D + D].rearrange("p (g h e) -> p g h e", h=2, e=DH)
                    hi, lo = (w[:, k, :, :].rearrange("p g (h r e) -> p g h r e", h=2, e=DH) for w in (wqk_h, wqk_l))
                    for r in range(3):
                        dve.tensor_copy(hi[:, :, :, r, :], src).then_inc(small_step, 1)
                        dve.wait_ge(small_step, 4 + 3 * k + r + 1)
                        dve.tensor_tensor(lo[:, :, :, r, :], src, hi[:, :, :, r, :].bitcast(F32),
                                          ALU.subtract).then_inc(small_w, 1)
                dve.tensor_copy(wvh[:, :], wqkv_s[:, 2 * D:3 * D]).then_inc(small_step, 1)
                dve.tensor_copy(woh[:, :], wo_s).then_inc(small_step, 1)
                dve.wait_ge(small_step, 12)
                dve.tensor_tensor(wvl[:, :], wqkv_s[:, 2 * D:3 * D], wvh[:, :].bitcast(F32), ALU.subtract).then_inc(small_w, 1)
                dve.tensor_tensor(wol[:, :], wo_s, woh[:, :].bitcast(F32), ALU.subtract).then_inc(small_w, 1)
                dve.wait_ge(small_w, 10)

            def first_misc(u):
                if u + 4 < len(parts):
                    split_part(u + 4)
                if u == 12:
                    attention_weights()

            def finish():
                f = ffn_number(FFN2, NB - 1)
                gate_y(f, 6)
                split_h(f, CHUNKS - 1)
                gate_y(f, 7)
                add_ffn2(NB - 1)

            slots(0, None, None, first_misc, None)
            pipeline(dve, phase_a, phase_b, finish)


_INS = ["x", "gamma", "wq", "wkv", "wo", "gw", "gb", "w1", "b1", "w2", "b2"]


def kernel(L0_attn_x, L0_attn_gamma, L0_attn_w_q, L0_attn_w_kv, L0_attn_w_out, L0_ffn_gate_w, L0_ffn_gate_b,
           L0_ffn_w1, L0_ffn_b1, L0_ffn_w2, L0_ffn_b2):
    import numpy as _np
    import concourse.bacc as _bacc
    from concourse.bass_utils import run_bass_kernel_spmd as _run

    arrays = {
        "x": L0_attn_x,
        "gamma": _np.reshape(L0_attn_gamma, (D, 1)),
        "wq": L0_attn_w_q,
        "wkv": L0_attn_w_kv,
        "wo": L0_attn_w_out,
        "gw": _np.transpose(L0_ffn_gate_w),
        "gb": L0_ffn_gate_b,
        "w1": L0_ffn_w1,
        "b1": _np.transpose(_np.reshape(L0_ffn_b1, (E * KC, P))),
        "w2": L0_ffn_w2,
        "b2": _np.transpose(L0_ffn_b2),
    }
    arrays = {f"in_{k}": _np.ascontiguousarray(a) for k, a in arrays.items()}
    nc = _bacc.Bacc("TRN2", target_bir_lowering=False, num_devices=1)
    args = [nc.dram_tensor(f"in_{k}", arrays[f"in_{k}"].shape, F32, kind="ExternalInput").ap() for k in _INS]
    out = nc.dram_tensor("out", (NB, T, D), F32, kind="ExternalOutput").ap()
    macaron(nc, *args, out)
    r = _run(nc, [arrays], core_ids=[0])
    return r.results[0]["out"]
```

```python
from contextlib import ExitStack

import concourse.bass as bass
from concourse import mybir

F32 = mybir.dt.float32
F32R = mybir.dt.float32r
ALU = mybir.AluOpType
ACT = mybir.ActivationFunctionType
AX_X = mybir.AxisListType.X

P = 128
NB, T, D = 8, 512, 128
TC = T // P
E, H = 8, 512
KC = H // P
CHUNKS = E * KC
UNITS = CHUNKS // 2
LAG = 4
HEADS, DH = 8, 16
VW = DH + 1
STEP = 64
LN_EPS, DEN_EPS, NORM_EPS = 1e-5, 1e-5, 1e-12
FFN1, FFN2 = 0, 1


def ffn_number(stage, j):
    if stage == FFN1:
        return 0 if isinstance(j, int) and j == 0 else j * 2 - 1
    return j * 2 + 2


def need(eng, sem=None, count=0):
    if not (isinstance(count, int) and count <= 0):
        eng.wait_ge(sem, count)


POOL_LO = (tuple(range(17)) + (20, 28, 30), tuple(c for c in range(CHUNKS) if c % 2 == 0 or c in (5, 11, 17, 23)))


def by_pool(s, c):
    return c in POOL_LO[s]


def lo_count(s, f, c):
    mine = [by_pool(s, x) == by_pool(s, c) for x in range(CHUNKS)]
    return f * sum(mine) + sum(mine[:c + 1])


def macaron(nc, x_d, gamma_d, wq_d, wkv_d, wo_d, gw_d, gb_d, w1_d, b1_d, w2_d, b2_d, out_d):
    with ExitStack() as ctx:
        def sb(name, shape, dt=F32):
            return ctx.enter_context(nc.sbuf_tensor(name, shape, dt))

        def pb(name, shape):
            return ctx.enter_context(nc.psum_tensor(name, shape, F32))

        def sem(name):
            return ctx.enter_context(nc.semaphore(name))

        w1h, w1l = sb("w1h", [P, E, H], F32R), sb("w1l", [P, E, H], F32R)
        w2h, w2l = sb("w2h", [P, E, KC, D], F32R), sb("w2l", [P, E, KC, D], F32R)
        b1c, b2c = sb("b1c", [P, E * KC]), sb("b2c", [P, E])
        gwf = sb("gwf", [P, E])
        gwh, gwl = sb("gwh", [P, E], F32R), sb("gwl", [P, E], F32R)
        gbb = sb("gbb", [P, E])
        wqk_h, wqk_l = sb("wqk_h", [P, 2, 4, P], F32R), sb("wqk_l", [P, 2, 4, P], F32R)
        wvh, wvl = sb("wvh", [P, D], F32R), sb("wvl", [P, D], F32R)
        woh, wol = sb("woh", [P, D], F32R), sb("wol", [P, D], F32R)
        gam = sb("gam", [P, 1])
        ident = sb("ident", [P, P])
        pick = sb("pick", [2 * E, E, P], F32R)
        rank = sb("rank", [P, TC, E])
        lomask = sb("lomask", [P, 2, 1])
        ones = sb("ones", [P, P], F32R)
        onef, mhalf, eps = sb("onef", [P, 1]), sb("mhalf", [P, TC]), sb("eps", [P, TC])
        idle = sb("idle", [P, 2])
        x0, x1, x2 = sb("x0", [P, TC, D]), sb("x1", [P, TC, D]), sb("x2", [P, TC, D])
        xn = sb("xn", [P, TC, D])
        stats, mv = sb("stats", [P, TC, 6]), sb("mv", [P, TC, 2])
        rstd, rms = sb("rstd", [P, TC]), sb("rms", [P, TC])
        xTh = [sb(f"xTh{s}", [P, T], F32R) for s in range(2)]
        xTl = [sb(f"xTl{s}", [P, T], F32R) for s in range(2)]
        hf = sb("hf", [P, LAG, T])
        hh = sb("hh", [P, 2 * LAG, T], F32R)
        hl = sb("hl", [P, LAG, T], F32R)
        gate, gy, acc = sb("gate", [P, T]), sb("gy", [P, T]), sb("acc", [P, T])
        lg, pr, pr2, tmp = (sb(n, [P, TC, E]) for n in ("lg", "pr", "pr2", "tmp"))
        f1, f2 = sb("f1", [P, TC, E]), sb("f2", [P, TC, E])
        red, rcp = sb("red", [P, TC]), sb("rcp", [P, TC])
        gcat = [sb(f"gcat{s}", [P, TC, 2 * E]) for s in range(2)]
        gTs = [sb(f"gTs{s}", [2 * E, T], F32R) for s in range(2)]
        nTh, nTl = sb("nTh", [P, T], F32R), sb("nTl", [P, T], F32R)
        qk = sb("qk", [P, 2, 4, T], F32R)
        vp = sb("vp", [P, TC, HEADS * 2 * VW + P - 2 * VW], F32R)
        vps = vp[:, :, 0:HEADS * 2 * VW].rearrange("p c (h v) -> p c h v", v=2 * VW)
        vsum = sb("vsum", [P, HEADS, VW])
        Pf = sb("Pf", [P, 2, 2, T])
        Ph, Pl = sb("Ph", [P, 4, 2, T], F32R), sb("Pl", [P, 2, 2, T], F32R)
        osb = sb("osb", [2 * VW, 2, T])
        nsum, nrec = sb("nsum", [P, 2, TC, VW]), sb("nrec", [P, 2, TC, 1])
        on = sb("on", [P, TC, D])

        z = pb("z", [P, 2, T])
        y = pb("y", [P, 2, T])
        G = pb("G", [P, T])
        S = pb("S", [P, 2, T])
        O = pb("O", [P, T])

        x_loaded, w_loaded = sem("x_loaded"), [sem(f"w_loaded{k}") for k in range(4)]
        ffn_loaded, attn_loaded, stored = sem("ffn_loaded"), sem("attn_loaded"), sem("stored")
        zeroed, cst, cst_dve = sem("zeroed"), sem("cst"), sem("cst_dve")
        w_hi, w_lo, small_w, small_step = sem("w_hi"), sem("w_lo"), sem("small_w"), sem("small_step")
        z_done, relu_done, h_hi = sem("z_done"), sem("relu_done"), sem("h_hi")
        h_lo = {True: sem("h_lo_pool"), False: sem("h_lo_dve")}
        y_part, gbc_full, gy_done, acc_done = sem("y_part"), sem("gbc_full"), sem("gy_done"), sem("acc_done")
        gate_ready = sem("gate_ready")
        accT_full, x1_ready, out_ready = sem("accT_full"), sem("x1_ready"), sem("out_ready")
        rstd_ready, rms_step = [sem(f"rstd_ready{s}") for s in range(3)], [sem(f"rms_step{s}") for s in range(3)]
        rms_done = sem("rms_done")
        ln_step, xn_ready = [sem(f"ln_step{s}") for s in range(3)], [sem(f"xn_ready{s}") for s in range(3)]
        xT_full, xT_hi, xT_lo = ([sem(f"{n}{s}") for s in range(3)] for n in ("xT_full", "xT_hi", "xT_lo"))
        logit_full, shifted, exp_done, gate_step, gates_ready, gT_full, gT_ready = (
            [sem(f"{n}{s}") for s in range(2)] for n in
            ("logit_full", "shifted", "exp_done", "gate_step", "gates_ready", "gT_full", "gT_ready"))
        v_full, v_hi, v_lo, vsum_full, vsum_hi, vsum_ready = (
            sem(n) for n in ("v_full", "v_hi", "v_lo", "vsum_full", "vsum_hi", "vsum_ready"))
        qk_full, qk_hi, qk_ready = sem("qk_full"), sem("qk_hi"), sem("qk_ready")
        s_full, p_full, p_lo, pv_done = (sem(n) for n in ("s_full", "p_full", "p_lo", "pv_done"))
        p_hi = [sem("p_hi_even"), sem("p_hi_odd")]
        o_ready, oT_full, norm_step, norm_done = (sem(n) for n in ("o_ready", "oT_full", "norm_step", "norm_done"))
        onT_full, onT_hi, onT_lo, proj_full, x2_ready = (
            sem(n) for n in ("onT_full", "onT_hi", "onT_lo", "proj_full", "x2_ready"))

        stage = Pf[:, :, :, :].rearrange("p a b t -> p (a b) t")
        parts = [(w, e) for e in range(E) for w in (1, 2)]
        part_hi = [w1h[:, e, :] if w == 1 else w2h[:, e, :, :].rearrange("p k d -> p (k d)") for w, e in parts]
        part_lo = [w1l[:, e, :] if w == 1 else w2l[:, e, :, :].rearrange("p k d -> p (k d)") for w, e in parts]
        wqkv_s = x1[:, :, :].rearrange("p c d -> p (c d)")[:, 0:3 * D]
        wo_s = x2[:, 0, :]
        NORM_STEPS = 4
        LN_STEPS = 2 * TC
        GATE_A, GATE_B = 9, 10

        def lo_ready(eng, s, f, c):
            if c < 0:
                f, c = f - 1, CHUNKS + c
            if not (isinstance(f, int) and f < 0):
                eng.wait_ge(h_lo[by_pool(s, c)], lo_count(s, f, c))

        block = ctx.enter_context(nc.Block())

        def pipeline(eng, phase_a, phase_b, finish):
            phase_b(0)
            for i in (1,):
                phase_a(i)
                phase_b(i)
            with eng.Fori(2, NB - 1) as i:
                phase_a(i)
                phase_b(i)
            phase_a(NB - 1)
            phase_b(NB - 1)
            phase_a(NB)
            phase_b(NB)
            finish()

        def is_last(i):
            return isinstance(i, int) and i == NB

        def prepared(i):
            return (FFN1, NB) if is_last(i) else (FFN2, i - 1)

        def ffn_of_a(i):
            s, j = (FFN2, NB - 2) if is_last(i) else (FFN1, i)
            return s, j, ffn_number(s, j)

        def before_a(i):
            return None if isinstance(i, int) and (i < 2 or i == NB) else ffn_number(FFN2, i - 2)

        def ffn_of_b(i):
            s, j = prepared(i)
            return s, j, None if isinstance(i, int) and i in (0, NB - 1) else ffn_number(s, j)

        def before_b(i):
            return ffn_number(FFN2, NB - 2) if is_last(i) else ffn_number(FFN1, i)

        @block.sync
        def _(sp):
            def load_x(j):
                if not (isinstance(j, int) and j == 0):
                    need(sp, x1_ready, j)
                sp.dma_start(x0[:, :, :], x_d[j, :, :].rearrange("(p c) d -> p c d", c=TC)).then_inc(x_loaded, 16)

            load_x(0)
            sp.dma_start(gwf[:, :], gw_d).then_inc(ffn_loaded, 16)
            sp.dma_start(gbb[:, :], gb_d.partition_broadcast(P)).then_inc(ffn_loaded, 16)
            sp.dma_start(b1c[:, :], b1_d).then_inc(ffn_loaded, 16)
            sp.dma_start(b2c[:, :], b2_d).then_inc(ffn_loaded, 16)
            for n, (w, e) in enumerate(parts):
                need(sp, w_lo, n - 3)
                if w == 1:
                    sp.dma_start(stage[:, n % 4, :], w1_d[e, :, :]).then_inc(w_loaded[n % 4], 16)
                else:
                    sp.dma_start(stage[:, n % 4, :].rearrange("p (k d) -> p k d", k=KC),
                                 w2_d[e, :, :].rearrange("(k p) d -> p k d", p=P)).then_inc(w_loaded[n % 4], 16)
                if n == 3:
                    sp.dma_start(gam[:, :], gamma_d).then_inc(attn_loaded, 16)
                    sp.dma_start(wqkv_s[:, 0:D], wq_d).then_inc(attn_loaded, 16)
                    sp.dma_start(wqkv_s[:, D:3 * D], wkv_d).then_inc(attn_loaded, 16)
                    sp.dma_start(wo_s, wo_d).then_inc(attn_loaded, 16)

            def store(j):
                sp.wait_ge(out_ready, j + 1)
                src = x0 if isinstance(j, int) and j == NB - 1 else x2
                sp.dma_start(out_d[j, :, :].rearrange("(p c) d -> p c d", c=TC), src[:, :, :]).then_inc(stored, 16)

            def phase_a(i):
                if not (isinstance(i, int) and i < 2):
                    store(i - 2)

            def phase_b(i):
                if not (isinstance(i, int) and i > NB - 2):
                    load_x(i + 1)

            pipeline(sp, phase_a, phase_b, lambda: store(NB - 1))
            sp.wait_ge(stored, 16 * NB)

        @block.gpsimd
        def _(pool):
            pool.memset(ident[:, :], 0.0).then_inc(zeroed, 1)
            pool.memset(hf[0:2 * E, 0:2, :], 0.0).then_inc(zeroed, 1)
            pool.memset(ones[:, :].bitcast(F32), 1.0).then_inc(cst, 1)
            pool.memset(onef[:, :], 1.0).then_inc(cst, 1)
            pool.memset(mhalf[:, :], -0.5).then_inc(zeroed, 1)
            pool.memset(eps[:, :], LN_EPS).then_inc(zeroed, 1)
            for e in range(E):
                pool.memset(rank[:, :, e:e + 1], float(E - e)).then_inc(cst, 1)
            pool.memset(vp[:, :, :].bitcast(F32), 0.0).then_inc(zeroed, 1)
            pool.wait_ge(zeroed, 1)
            pool.affine_select(out=ident[:, :], in_=ident[:, :], compare_op=ALU.not_equal, fill=1.0, base=0,
                               pattern=[[-1, P]], channel_multiplier=1).then_inc(cst, 1)
            pool.wait_ge(zeroed, 2)
            pk = hf[0:2 * E, 0:2, :].rearrange("k a t -> k (a t)").rearrange("k (e p) -> k e p", e=E)
            pool.affine_select(out=pk, in_=pk, compare_op=ALU.not_equal, fill=1.0, base=0,
                               pattern=[[-1, E], [0, P]], channel_multiplier=1).then_inc(zeroed, 1)
            pool.wait_ge(zeroed, 6)
            pool.affine_select(out=pk, in_=pk, compare_op=ALU.not_equal, fill=1.0, base=-E,
                               pattern=[[-1, E], [0, P]], channel_multiplier=1).then_inc(cst, 1)
            pool.wait_ge(zeroed, 5)
            pool.memset(vps[:, :, :, DH:VW].bitcast(F32), 1.0).then_inc(cst, 1)

            def split_h(s, f, c):
                pool.wait_ge(h_hi, f * CHUNKS + c + 1)
                need(pool, y_part, f * CHUNKS + c - LAG + 1)
                pool.tensor_tensor(hl[:, c % LAG, :], hf[:, c % LAG, :], hh[:, c % (2 * LAG), :].bitcast(F32),
                                   ALU.subtract).then_inc(h_lo[True], 1)

            def add_gated(f, e):
                pool.wait_ge(gy_done, f * 8 + e + 1)
                need(pool, acc_done, f * 7 + e - 1)
                pool.tensor_tensor(acc[:, :], acc[:, :], gy[:, :], ALU.add).then_inc(acc_done, 1)

            def inverse_deviation(s, j):
                pool.wait_ge(ln_step[s], (j + 1) * LN_STEPS)
                step = rms_step[s]
                n = j * (5 if s == 2 else 1)
                pool.tensor_tensor(rstd[:, :], mv[:, :, 1], eps[:, :], ALU.add).then_inc(step, 1)
                pool.wait_ge(step, n + 1)
                last = pool.tensor_tensor(rstd[:, :], rstd[:, :], mhalf[:, :], ALU.pow)
                if s == 2:
                    last.then_inc(step, 1)
                    pool.wait_ge(step, n + 2)
                    pool.tensor_tensor(rms[:, :], mv[:, :, 1], rstd[:, :], ALU.mult).then_inc(step, 1)
                    pool.wait_ge(step, n + 3)
                    pool.tensor_tensor(rms[:, :], rms[:, :], rstd[:, :], ALU.mult).then_inc(step, 1)
                    pool.wait_ge(step, n + 4)
                    pool.tensor_tensor(idle[:, 0:1], eps[:, 0:1], eps[:, 0:1], ALU.add)
                    pool.tensor_scalar(rms[:, :], rms[:, :], NORM_EPS ** 2 / D, None, ALU.max).then_inc(step, 1)
                    pool.wait_ge(step, n + 5)
                    pool.tensor_tensor(rms[:, :], rms[:, :], mhalf[:, :], ALU.pow).then_inc(rms_done, 1)
                    pool.wait_ge(rms_done, j + 1)
                    last = pool.tensor_tensor(rstd[:, :], rms[:, :], rstd[:, :], ALU.mult)
                last.then_inc(rstd_ready[s], 1)

            def slots(s, f, before, norms):
                for u in range(UNITS):
                    if u in norms:
                        inverse_deviation(*norms[u])
                    if before is not None and u in (0, 2):
                        add_gated(before, 6 + u // 2)
                    if f is not None:
                        if u >= 6 and u % 2 == 0:
                            add_gated(f, u // 2 - 2)
                        for c in (2 * u, 2 * u + 1):
                            if by_pool(s, c):
                                split_h(s, f, c)

            def phase_a(i):
                s, _, f = ffn_of_a(i)
                slots(s, f, before_a(i), {13: prepared(i)})

            def phase_b(i):
                s, _, f = ffn_of_b(i)
                norms = {} if is_last(i) else {5: (2, i)}
                if not (isinstance(i, int) and i >= NB - 1):
                    norms[8] = (FFN1, i + 1)
                slots(s, f, before_b(i), norms)

            inverse_deviation(FFN1, 0)
            slots(FFN1, 0, None, {})
            pipeline(pool, phase_a, phase_b, lambda: slots(FFN1, None, ffn_number(FFN1, NB), {}))

        @block.scalar
        def _(act):
            def relu(s, f, u, cc):
                c = 2 * u + cc
                act.wait_ge(z_done, f * 32 + c + 1)
                lo_ready(act, s, f, c - LAG)
                act.activation(hf[:, c % LAG, :], z[:, c % 2, :], ACT.Relu,
                               bias=b1c[:, c:c + 1]).then_inc(relu_done, 1)

            def copy_gate(f, e):
                act.wait_ge(gbc_full, f * 8 + e + 1)
                need(act, gy_done, f * 8 + e)
                act.activation(gate[:, :], G[:, :], ACT.Copy).then_inc(gate_ready, 1)

            def squares(j, p):
                act.wait_ge(s_full, j * 16 + p + 1)
                if p % 2 == 0:
                    need(act, pv_done, j * 16 + p - 3)
                    act.activation(Ph[:, p % 4, :, :], S[:, :, :], ACT.Square, bias=onef[:, :]).then_inc(p_hi[0], 1)
                need(act, p_lo, j * 16 + p - 1)
                if p < 2:
                    need(act, qk_ready, j * 8 + 8)
                act.activation(Pf[:, p % 2, :, :], S[:, :, :], ACT.Square, bias=onef[:, :]).then_inc(p_full, 1)

            def head_out(j, h):
                act.wait_ge(pv_done, j * 16 + 2 * h + 2)
                need(act, oT_full, j * 4 + h // 2)
                act.activation(osb[:, h % 2, :], O[0:2 * VW, :], ACT.Copy).then_inc(o_ready, 1)

            def round_xT(s, j, bank):
                act.wait_ge(xT_full[s], j + 1)
                if s == 2:
                    need(act, proj_full, j)
                elif not (isinstance(j, int) and j == 0):
                    act.wait_ge(z_done, ffn_number(s, j - 1) * 32 + 32)
                dst = nTh if s == 2 else xTh[s]
                act.activation(dst[:, :], bank, ACT.Copy).then_inc(xT_hi[s], 1)

            def exps(s, j):
                act.wait_ge(shifted[s], j + 1)
                act.activation(tmp[:, :, :], lg[:, :, :], ACT.Exp).then_inc(exp_done[s], 1)

            def copy_gT(s, j, bank):
                act.wait_ge(gT_full[s], j + 1)
                if not (isinstance(j, int) and j == 0):
                    act.wait_ge(gbc_full, ffn_number(s, j - 1) * 8 + 8)
                act.activation(gTs[s][:, :], bank[0:2 * E, :], ACT.Copy).then_inc(gT_ready[s], 1)

            def slots(s, f, heads, before, misc):
                for u in range(UNITS):
                    h = u - 1
                    if heads is not None and 0 <= h < HEADS:
                        squares(heads, 2 * h)
                    if f is not None:
                        relu(s, f, u, 0)
                    if heads is not None and 0 <= h < HEADS:
                        squares(heads, 2 * h + 1)
                    if f is not None:
                        relu(s, f, u, 1)
                    if heads is not None and 1 <= h <= HEADS:
                        head_out(heads, h - 1)
                    if before is not None and u == 1:
                        copy_gate(before, 7)
                    if f is not None and u >= 3 and u % 2 == 1:
                        copy_gate(f, (u - 3) // 2)
                    misc(u)

            def phase_a(i):
                def misc(u):
                    j = i - 1
                    if u == 11:
                        act.wait_ge(onT_full, j + 1)
                        act.wait_ge(qk_full, (j + 1) * 8)
                        act.activation(nTh[:, :], S[:, 0, :], ACT.Copy).then_inc(onT_hi, 1)
                    if u == 14:
                        round_xT(*prepared(i), S[:, 0, :])
                    if u == 15:
                        exps(*prepared(i))

                s, _, f = ffn_of_a(i)
                slots(s, f, i - 1, before_a(i), misc)

            def phase_b(i):
                def misc(u):
                    if u == 2 and not (isinstance(i, int) and i == 0):
                        copy_gT(*prepared(i), S[:, 1, :])
                    if is_last(i):
                        return
                    if u == 7:
                        round_xT(2, i, O[:, :])
                    if u == 8:
                        act.wait_ge(v_full, i + 1)
                        need(act, pv_done, i * 16)
                        act.activation(vps[:, :, :, 0:DH], S[:, 0, :].rearrange("p (c h e) -> p c h e", c=TC, h=HEADS),
                                       ACT.Copy).then_inc(v_hi, 1)
                    if 10 <= u < 14:
                        for t in range(2 * (u - 10), 2 * (u - 10) + 2):
                            act.wait_ge(qk_full, i * 8 + t + 1)
                            if t >= 2:
                                act.wait_ge(qk_ready, i * 8 + t - 1)
                            else:
                                need(act, p_lo, i * 16)
                            act.activation(Pf[:, t % 2, 0, :].bitcast(F32R), S[:, t % 2, :],
                                           ACT.Copy).then_inc(qk_hi, 1)
                    if isinstance(i, int) and i == NB - 1:
                        return
                    if u == 9:
                        round_xT(FFN1, i + 1, O[:, :])
                    if u == 10:
                        exps(FFN1, i + 1)
                    if u == 13:
                        copy_gT(FFN1, i + 1, O[:, :])

                s, _, f = ffn_of_b(i)
                slots(s, f, None, before_b(i), misc)

            def round_part(n):
                act.wait_ge(w_loaded[n % 4], 16 * (n // 4 + 1))
                act.activation(part_hi[n], stage[:, n % 4, :], ACT.Copy).then_inc(w_hi, 1)

            for n in range(4):
                round_part(n)
                if n == 0:
                    round_xT(FFN1, 0, O[:, :])
                if n == 1:
                    exps(FFN1, 0)
                if n == 2:
                    copy_gT(FFN1, 0, O[:, :])
                    act.wait_ge(cst, 2)
            act.wait_ge(cst_dve, 1)
            act.wait_ge(ffn_loaded, 16 * 4)
            slots(FFN1, 0, None, None, lambda u: round_part(u + 4) if u + 4 < len(parts) else None)
            act.wait_ge(w_lo, len(parts))
            pipeline(act, phase_a, phase_b, lambda: copy_gate(ffn_number(FFN1, NB), 7))

        @block.tensor
        def _(pe):
            def three(out, a_hi, a_lo, b_hi, b_lo, start, stop):
                pe.matmul(out, a_hi, b_hi, start=start, stop=False)
                pe.matmul(out, a_hi, b_lo, start=False, stop=False)
                return pe.matmul(out, a_lo, b_hi, start=False, stop=stop)

            def mm1(s, f, u, cc):
                c = 2 * u + cc
                k = c % KC
                if isinstance(f, int) and f == 0 and cc == 0 and u % 2 == 0:
                    pe.wait_ge(w_lo, u + 1)
                need(pe, relu_done, f * 32 + c - 1)
                w = slice(k * P, k * P + P)
                three(z[:, c % 2, :], w1h[:, u // 2, w], w1l[:, u // 2, w], xTh[s][:, :], xTl[s][:, :],
                      True, True).then_inc(z_done, 1)

            def mm2(s, f, c):
                e, k = c // KC, c % KC
                if isinstance(f, int) and f == 0 and k == 0:
                    pe.wait_ge(w_lo, 2 * e + 2)
                lo_ready(pe, s, f, c)
                if k == 0:
                    need(pe, gy_done, f * 8 + e - 1)
                three(y[:, e % 2, :], w2h[:, e, k, :], w2l[:, e, k, :], hh[:, c % (2 * LAG), :], hl[:, c % LAG, :],
                      k == 0, k == KC - 1).then_inc(y_part, 1)

            def spread_gate(s, j, f, e):
                if e == 0:
                    pe.wait_ge(gT_ready[s], j + 1)
                need(pe, gate_ready, f * 8 + e)
                pe.matmul(G[:, :], pick[:, e, :], gTs[s][:, :], start=True, stop=True).then_inc(gbc_full, 1)

            def transpose_sum(f):
                pe.wait_ge(acc_done, f * 7 + 7)
                pe.wait_ge(gate_ready, f * 8 + 8)
                for c in range(TC):
                    mm = pe.transpose(G[:, c * P:c * P + P], acc[:, c * P:c * P + P], ident[:, :])
                mm.then_inc(accT_full, 1)

            def scores(j, p):
                h = p // 2
                if p == 0:
                    pe.wait_ge(qk_ready, j * 8 + 8)
                need(pe, p_full, j * 16 + p)
                rows = slice(STEP * (h % 2), STEP * (h % 2) + STEP)
                for mc in range(2):
                    m = 2 * (p % 2) + mc
                    mm = pe.matmul(S[:, mc, :], qk[rows, 1, h // 2, m * P:m * P + P], qk[rows, 0, h // 2, :],
                                   start=True, stop=True)
                mm.then_inc(s_full, 1)

            def weigh(j, p):
                h = p // 2
                pe.wait_ge(p_lo, j * 16 + p + 1)
                if p % 2 == 0:
                    need(pe, o_ready, j * 8 + h)
                for mc in range(2):
                    m = 2 * (p % 2) + mc
                    v = vp[:, m, h * 2 * VW:h * 2 * VW + P]
                    pe.matmul(O[:, :], v, Ph[:, p % 4, mc, :], start=(m == 0), stop=False)
                    mm = pe.matmul(O[:, :], v, Pl[:, p % 2, mc, :], start=False, stop=(m == TC - 1))
                mm.then_inc(pv_done, 1)

            def transpose_heads(j, hp, free):
                pe.wait_ge(o_ready, j * 8 + 2 * hp + 2)
                need(pe, *free)
                pe.matmul(G[:, 0:1], ident[:, :], ident[:, 0:1], start=True, stop=True)
                for h in range(2):
                    for c in range(TC):
                        at = (h * TC + c) * 2 * VW
                        mm = pe.transpose(G[:, at:at + 2 * VW], osb[:, h, c * P:c * P + P], ident[0:2 * VW, 0:2 * VW])
                mm.then_inc(oT_full, 1)

            def transpose_xn(s, j, bank):
                pe.wait_ge(xn_ready[s], j + 1)
                for c in range(TC):
                    mm = pe.transpose(bank[:, c * P:c * P + P], xn[:, c, :], ident[:, :])
                mm.then_inc(xT_full[s], 1)

            def logits(s, j, bank):
                pe.wait_ge(xT_hi[s], j + 1)
                pe.wait_ge(xT_lo[s], j + 1)
                for c in range(TC):
                    tok = slice(c * P, c * P + P)
                    mm = three(bank[:, c * E:c * E + E], xTh[s][:, tok], xTl[s][:, tok], gwh[:, :], gwl[:, :], True, True)
                mm.then_inc(logit_full[s], 1)

            def transpose_gates(s, j, bank):
                pe.wait_ge(gates_ready[s], j + 1)
                for c in range(TC):
                    mm = pe.transpose(bank[0:2 * E, c * P:c * P + P], gcat[s][:, c, :], ident[:, :])
                mm.then_inc(gT_full[s], 1)

            def slots(s, j, f, heads, before, residual, misc):
                for u in range(UNITS):
                    def second(cc):
                        c = 2 * u + cc - LAG
                        if c < 0:
                            if before is not None:
                                mm2(1 - s, before, CHUNKS + c)
                        elif f is not None:
                            mm2(s, f, c)

                    h = u - 1
                    if heads is not None and 0 <= h < HEADS:
                        scores(heads, 2 * h)
                    if f is not None:
                        mm1(s, f, u, 0)
                    if u == 1 and before is not None:
                        spread_gate(1 - s, None, before, 7)
                    if u >= 5 and u % 2 == 1 and u != 11 and f is not None:
                        if heads is not None and u < 11:
                            pe.wait_ge(norm_done, heads * 4 + (u - 3) // 2)
                        spread_gate(s, j, f, (u - 3) // 2)
                    second(0)
                    if u == 3 and before is not None:
                        transpose_sum(before)
                    if heads is not None and 4 <= u <= 10 and u % 2 == 0:
                        free = (gate_ready, f * 8 + (u - 2) // 2) if f is not None else residual if u == 4 else ()
                        transpose_heads(heads, (u - 4) // 2, free)
                    if heads is not None and 1 <= h <= HEADS:
                        weigh(heads, 2 * h - 2)
                    if heads is not None and 0 <= h < HEADS:
                        scores(heads, 2 * h + 1)
                    if f is not None:
                        mm1(s, f, u, 1)
                    second(1)
                    if heads is not None and 1 <= h <= HEADS:
                        weigh(heads, 2 * h - 1)
                    if u == 11 and f is not None:
                        if heads is not None:
                            pe.wait_ge(norm_done, heads * 4 + 4)
                        spread_gate(s, j, f, 4)
                    if u == 3 and f is not None:
                        need(pe, *residual)
                        spread_gate(s, j, f, 0)
                    misc(u)

            def phase_a(i):
                def misc(u):
                    j = i - 1
                    if u == 11:
                        pe.wait_ge(norm_done, j * 4 + 4)
                        pe.wait_ge(p_full, j * 16 + 16)
                        for c in range(TC):
                            mm = pe.transpose(S[:, 0, c * P:c * P + P], on[:, c, :], ident[:, :])
                        mm.then_inc(onT_full, 1)
                    if u == 12:
                        pe.wait_ge(onT_hi, j + 1)
                        pe.wait_ge(onT_lo, j + 1)
                        for c in range(TC):
                            tok = slice(c * P, c * P + P)
                            mm = three(O[:, tok], nTh[:, tok], nTl[:, tok], woh[:, :], wol[:, :], True, True)
                        mm.then_inc(proj_full, 1)
                    if u == 14:
                        transpose_xn(*prepared(i), S[:, 0, :])
                    if u == 15:
                        logits(*prepared(i), S[:, 1, :])

                before = before_a(i)
                slots(*ffn_of_a(i), i - 1, before, () if before is None else (out_ready, i - 1), misc)

            def phase_b(i):
                def misc(u):
                    if u == 2 and not (isinstance(i, int) and i == 0):
                        transpose_gates(*prepared(i), S[:, 1, :])
                    if is_last(i):
                        return
                    if u == 7:
                        need(pe, x2_ready, i)
                        transpose_xn(2, i, O[:, :])
                    if u == 8:
                        pe.wait_ge(xT_hi[2], i + 1)
                        pe.wait_ge(xT_lo[2], i + 1)
                        need(pe, gT_ready[FFN2], i)
                        for c in range(TC):
                            tok = slice(c * P, c * P + P)
                            mm = three(S[:, 0, tok], nTh[:, tok], nTl[:, tok], wvh[:, :], wvl[:, :], True, True)
                        mm.then_inc(v_full, 1)
                    if u == 9:
                        pe.wait_ge(v_hi, i + 1)
                        pe.wait_ge(v_lo, i + 1)
                        for c in range(TC):
                            mm = pe.matmul(S[:, 1, 0:HEADS * 2 * VW], ones[:, :], vp[:, c, 0:HEADS * 2 * VW],
                                           start=(c == 0), stop=(c == TC - 1))
                        mm.then_inc(vsum_full, 1)
                    if 10 <= u < 14:
                        for t in range(2 * (u - 10), 2 * (u - 10) + 2):
                            if t == 1:
                                pe.wait_ge(vsum_ready, i + 1)
                            if t >= 2:
                                pe.wait_ge(qk_ready, i * 8 + t - 1)
                            three(S[:, t % 2, :], wqk_h[:, t % 2, t // 2, :], wqk_l[:, t % 2, t // 2, :],
                                  nTh[:, :], nTl[:, :], True, True).then_inc(qk_full, 1)
                    if isinstance(i, int) and i == NB - 1:
                        return
                    if u == 9:
                        transpose_xn(FFN1, i + 1, O[:, :])
                    if u == 10:
                        logits(FFN1, i + 1, O[:, :])
                    if u == 13:
                        transpose_gates(FFN1, i + 1, O[:, :])

                slots(*ffn_of_b(i), None, before_b(i), (out_ready, NB - 1) if is_last(i) else (x1_ready, i + 1), misc)

            def finish():
                f = ffn_number(FFN1, NB)
                for u in range(2):
                    for cc in range(2):
                        mm2(FFN1, f, CHUNKS - LAG + 2 * u + cc)
                    if u == 0:
                        spread_gate(FFN1, NB, f, 7)
                transpose_sum(f)

            pe.wait_ge(cst, 11)
            transpose_xn(FFN1, 0, O[:, :])
            pe.wait_ge(small_w, 2)
            logits(FFN1, 0, O[:, :])
            transpose_gates(FFN1, 0, O[:, :])
            pe.wait_ge(cst_dve, 1)
            slots(FFN1, 0, 0, None, None, (), lambda u: None)
            pe.wait_ge(small_w, 10)
            pipeline(pe, phase_a, phase_b, finish)

        @block.vector
        def _(dve):
            def bc(ap, n):
                return ap.unsqueeze(2).to_broadcast([P, TC, n])

            def split_h(s, f, c):
                dve.wait_ge(relu_done, f * CHUNKS + c + 1)
                need(dve, y_part, f * CHUNKS + c - 2 * LAG + 1)
                dve.tensor_copy(hh[:, c % (2 * LAG), :], hf[:, c % LAG, :]).then_inc(h_hi, 1)
                if not by_pool(s, c):
                    dve.wait_ge(h_hi, f * CHUNKS + c + 1)
                    need(dve, y_part, f * CHUNKS + c - LAG + 1)
                    dve.tensor_tensor(hl[:, c % LAG, :], hf[:, c % LAG, :], hh[:, c % (2 * LAG), :].bitcast(F32),
                                      ALU.subtract).then_inc(h_lo[False], 1)

            def gate_y(f, e):
                dve.wait_ge(y_part, f * CHUNKS + KC * (e + 1))
                dve.wait_ge(gate_ready, f * 8 + e + 1)
                if e == 0:
                    need(dve, accT_full, f)
                else:
                    need(dve, acc_done, f * 7 + e - 1)
                dve.scalar_tensor_tensor(acc[:, :] if e == 0 else gy[:, :], y[:, e % 2, :], b2c[:, e:e + 1], gate[:, :],
                                         ALU.add, ALU.mult).then_inc(gy_done, 1)

            def split_p(j, p):
                dve.wait_ge(p_full, j * 16 + p + 1)
                if p % 2 == 1:
                    need(dve, pv_done, j * 16 + p - 3)
                    dve.tensor_copy(Ph[:, p % 4, :, :], Pf[:, p % 2, :, :]).then_inc(p_hi[1], 1)
                    dve.wait_ge(p_hi[1], j * 8 + p // 2 + 1)
                need(dve, pv_done, j * 16 + p - 1)
                dve.tensor_tensor(Pl[:, p % 2, :, :], Pf[:, p % 2, :, :], Ph[:, p % 4, :, :].bitcast(F32),
                                  ALU.subtract).then_inc(p_lo, 1)

            def statistics(s, j, src):
                for c in range(TC):
                    dve.bn_stats(stats[:, c, :], src[:, c, :]).then_inc(ln_step[s], 1)
                dve.wait_ge(ln_step[s], j * LN_STEPS + TC)
                dve.memset(idle[:, 1:2], 0.0)
                for c in range(TC):
                    dve.bn_aggr(mv[:, c, :], stats[:, c, :]).then_inc(ln_step[s], 1)

            def layer_norm(s, j, src):
                dve.wait_ge(rstd_ready[s], j + 1)
                if s == FFN1:
                    need(dve, xT_full[2], j)
                elif s == 2:
                    need(dve, xT_full[FFN2], j)
                    need(dve, xT_full[FFN1], j + 1)
                else:
                    need(dve, xT_full[FFN1], j + 2 if not (isinstance(j, int) and j == NB - 1) else NB)
                    need(dve, xT_full[2], j + 1)
                for c in range(TC):
                    ins = dve.tensor_scalar(xn[:, c, :], src[:, c, :], mv[:, c, 0:1], rstd[:, c:c + 1],
                                            ALU.subtract, ALU.mult)
                ins.then_inc(xn_ready[s], 1)

            def split_xT(s, j, bank):
                dve.wait_ge(xT_hi[s], j + 1)
                hi, lo = (nTh, nTl) if s == 2 else (xTh[s], xTl[s])
                dve.tensor_tensor(lo[:, :], bank, hi[:, :].bitcast(F32), ALU.subtract).then_inc(xT_lo[s], 1)

            def shift_logits(s, j, bank):
                n = j * (GATE_A + GATE_B)
                dve.wait_ge(logit_full[s], j + 1)
                dve.tensor_tensor(pr2[:, :, :], bank[:, 0:TC * E].rearrange("p (c e) -> p c e", e=E),
                                  gbb[:, :].unsqueeze(1).to_broadcast([P, TC, E]), ALU.add).then_inc(gate_step[s], 1)
                dve.wait_ge(gate_step[s], n + 1)
                dve.tensor_reduce(red[:, :], pr2[:, :, :], AX_X, ALU.max).then_inc(gate_step[s], 1)
                dve.wait_ge(gate_step[s], n + 2)
                dve.tensor_tensor(lg[:, :, :], pr2[:, :, :], bc(red[:, :], E), ALU.subtract).then_inc(shifted[s], 1)

            def choose(s, n, values, out):
                dve.tensor_reduce(red[:, :], values[:, :, :], AX_X, ALU.max).then_inc(gate_step[s], 1)
                dve.wait_ge(gate_step[s], n + 1)
                dve.tensor_tensor(f2[:, :, :], values[:, :, :], bc(red[:, :], E), ALU.is_equal).then_inc(gate_step[s], 1)
                dve.wait_ge(gate_step[s], n + 2)
                dve.tensor_tensor(lg[:, :, :], f2[:, :, :], rank[:, :, :], ALU.mult).then_inc(gate_step[s], 1)
                dve.wait_ge(gate_step[s], n + 3)
                dve.tensor_reduce(red[:, :], lg[:, :, :], AX_X, ALU.max).then_inc(gate_step[s], 1)
                dve.wait_ge(gate_step[s], n + 4)
                dve.tensor_tensor(out[:, :, :], rank[:, :, :], bc(red[:, :], E), ALU.is_equal).then_inc(gate_step[s], 1)
                dve.wait_ge(gate_step[s], n + 5)

            def probabilities(s, j):
                n = j * (GATE_A + GATE_B) + 2
                dve.wait_ge(exp_done[s], j + 1)
                dve.tensor_reduce(red[:, :], tmp[:, :, :], AX_X, ALU.add).then_inc(gate_step[s], 1)
                dve.wait_ge(gate_step[s], n + 1)
                dve.reciprocal(rcp[:, :], red[:, :]).then_inc(gate_step[s], 1)
                dve.wait_ge(gate_step[s], n + 2)
                dve.tensor_tensor(pr[:, :, :], tmp[:, :, :], bc(rcp[:, :], E), ALU.mult).then_inc(gate_step[s], 1)
                dve.wait_ge(gate_step[s], n + 3)
                choose(s, n + 3, pr, f1)

            def top_two(s, j):
                n = j * (GATE_A + GATE_B) + 10
                dve.scalar_tensor_tensor(pr2[:, :, :], f1[:, :, :], -2.0, pr[:, :, :],
                                         ALU.mult, ALU.add).then_inc(gate_step[s], 1)
                dve.wait_ge(gate_step[s], n + 1)
                choose(s, n + 1, pr2, tmp)
                dve.tensor_tensor(f1[:, :, :], f1[:, :, :], tmp[:, :, :], ALU.add).then_inc(gate_step[s], 1)
                dve.wait_ge(gate_step[s], n + 7)
                dve.tensor_tensor(pr[:, :, :], pr[:, :, :], f1[:, :, :], ALU.mult).then_inc(gate_step[s], 1)
                dve.wait_ge(gate_step[s], n + 8)
                need(dve, gT_full[s], j)
                dve.tensor_copy(gcat[s][:, :, 0:E].bitcast(F32R), pr[:, :, :]).then_inc(gate_step[s], 1)
                dve.wait_ge(gate_step[s], n + 9)
                dve.tensor_tensor(gcat[s][:, :, E:2 * E].bitcast(F32R), pr[:, :, :], gcat[s][:, :, 0:E],
                                  ALU.subtract).then_inc(gates_ready[s], 1)

            def normalise(j, hp):
                n = (j * 4 + hp) * NORM_STEPS
                both = G[:, 0:4 * TC * VW].rearrange("p (h c v) -> p h c v", h=2, v=2 * VW)
                dve.wait_ge(oT_full, j * 4 + hp + 1)
                if hp == 0:
                    dve.wait_ge(vsum_ready, j + 1)
                dve.tensor_tensor(nsum[:, :, :, :], both[:, :, :, 0:VW],
                                  vsum[:, 2 * hp:2 * hp + 2, :].unsqueeze(2).to_broadcast([P, 2, TC, VW]),
                                  ALU.add).then_inc(norm_step, 1)
                dve.wait_ge(norm_step, n + 1)
                dve.tensor_tensor(nsum[:, :, :, :], nsum[:, :, :, :], both[:, :, :, VW:2 * VW],
                                  ALU.add).then_inc(norm_step, 1)
                dve.wait_ge(norm_step, n + 2)
                dve.tensor_scalar(nrec[:, :, :, :], nsum[:, :, :, DH:VW], 2 * DEN_EPS, None,
                                  ALU.max).then_inc(norm_step, 1)
                dve.wait_ge(norm_step, n + 3)
                dve.reciprocal(nrec[:, :, :, :], nrec[:, :, :, :]).then_inc(norm_step, 1)
                dve.wait_ge(norm_step, n + 4)
                if hp == 0:
                    need(dve, onT_full, j)
                ins = None
                for h in range(2):
                    head = 2 * hp + h
                    ins = dve.tensor_tensor(on[:, :, head * DH:head * DH + DH], nsum[:, h, :, 0:DH],
                                            nrec[:, h, :, :].to_broadcast([P, TC, DH]), ALU.mult)
                ins.then_inc(norm_done, 1)

            def slots(s, f, heads, before, misc, residual):
                for u in range(UNITS):
                    h = u - 1
                    if u in (0, 2) and before is not None:
                        gate_y(before, 6 + u // 2)
                    if u >= 4 and u % 2 == 0 and f is not None:
                        gate_y(f, u // 2 - 2)
                    if u > 0 and f is not None:
                        split_h(s, f, 2 * u - 1)
                    if u == 0 and before is not None:
                        split_h(1 - s, before, CHUNKS - 1)
                    if u == 3 and before is not None:
                        residual()
                    if heads is not None and 0 <= h < HEADS:
                        split_p(heads, 2 * h)
                    if f is not None:
                        split_h(s, f, 2 * u)
                    if heads is not None and 4 <= u <= 10 and u % 2 == 0:
                        normalise(heads, (u - 4) // 2)
                    if heads is not None and 0 <= h < HEADS:
                        split_p(heads, 2 * h + 1)
                    misc(u)

            def add_ffn2(f, x_in):
                dve.wait_ge(accT_full, f + 1)
                dve.scalar_tensor_tensor(x_in[:, :, :], G[:, :].rearrange("p (c d) -> p c d", c=TC), 0.5, x_in[:, :, :],
                                         ALU.mult, ALU.add).then_inc(out_ready, 1)

            def phase_a(i):
                x_in = x0 if is_last(i) else x2

                def misc(u):
                    j = i - 1
                    if u == 11:
                        dve.wait_ge(onT_hi, j + 1)
                        dve.tensor_tensor(nTl[:, :], S[:, 0, :], nTh[:, :].bitcast(F32),
                                          ALU.subtract).then_inc(onT_lo, 1)
                    if u == 12:
                        dve.wait_ge(proj_full, j + 1)
                        if not (isinstance(i, int) and (i < 2 or i == NB)):
                            dve.wait_ge(stored, (i - 1) * 16)
                        dve.tensor_tensor(x_in[:, :, :], O[:, :].rearrange("p (c d) -> p c d", c=TC), x1[:, :, :],
                                          ALU.add).then_inc(x2_ready, 1)
                        dve.wait_ge(x2_ready, j + 1)
                        statistics(*prepared(i), x_in)
                    if u == 13:
                        layer_norm(*prepared(i), x_in)
                    if u == 14:
                        split_xT(*prepared(i), S[:, 0, :])
                    if u == 15:
                        shift_logits(*prepared(i), S[:, 1, :])

                s, _, f = ffn_of_a(i)
                before = before_a(i)
                slots(s, f, i - 1, before, misc, lambda: add_ffn2(before, x2))

            def phase_b(i):
                def residual():
                    if is_last(i):
                        add_ffn2(before_b(i), x2)
                        return
                    dve.wait_ge(accT_full, ffn_number(FFN1, i) + 1)
                    dve.scalar_tensor_tensor(x1[:, :, :], G[:, :].rearrange("p (c d) -> p c d", c=TC), 0.5, x0[:, :, :],
                                             ALU.mult, ALU.add).then_inc(x1_ready, 1)

                def misc(u):
                    if u == 0 and not (isinstance(i, int) and i == 0):
                        probabilities(*prepared(i))
                    if u == 1 and not (isinstance(i, int) and i == 0):
                        top_two(*prepared(i))
                    if is_last(i):
                        return
                    if u == 4:
                        dve.wait_ge(x1_ready, i + 1)
                        statistics(2, i, x1)
                    if u == 6:
                        layer_norm(2, i, x1)
                    if u == 7:
                        split_xT(2, i, O[:, :])
                    if u == 8:
                        dve.wait_ge(v_hi, i + 1)
                        dve.tensor_tensor(vps[:, :, :, VW:VW + DH],
                                          S[:, 0, :].rearrange("p (c h e) -> p c h e", c=TC, h=HEADS),
                                          vps[:, :, :, 0:DH].bitcast(F32), ALU.subtract).then_inc(v_lo, 1)
                    if u == 9:
                        dve.wait_ge(vsum_full, i + 1)
                        sums = S[:, 1, 0:HEADS * 2 * VW].rearrange("p (h v) -> p h v", v=2 * VW)
                        dve.tensor_copy(vsum[:, :, :], sums[:, :, 0:VW]).then_inc(vsum_hi, 1)
                        dve.wait_ge(vsum_hi, i + 1)
                        dve.tensor_tensor(vsum[:, :, :], vsum[:, :, :], sums[:, :, VW:2 * VW],
                                          ALU.add).then_inc(vsum_ready, 1)
                    if 10 <= u < 14:
                        for t in range(2 * (u - 10), 2 * (u - 10) + 2):
                            dve.wait_ge(qk_hi, i * 8 + t + 1)
                            if t == 0:
                                need(dve, s_full, i * 16)
                            dve.scalar_tensor_tensor(qk[:, t % 2, t // 2, :], Pf[:, t % 2, 0, :],
                                                     lomask[:, t % 2, :], S[:, t % 2, :],
                                                     ALU.mult, ALU.add).then_inc(qk_ready, 1)
                    if isinstance(i, int) and i == NB - 1:
                        return
                    if u == 7:
                        dve.wait_ge(x_loaded, (i + 2) * 16)
                        statistics(FFN1, i + 1, x0)
                    if u == 8:
                        layer_norm(FFN1, i + 1, x0)
                    if u == 9:
                        split_xT(FFN1, i + 1, O[:, :])
                    if u == 10:
                        shift_logits(FFN1, i + 1, O[:, :])
                    if u == 11:
                        probabilities(FFN1, i + 1)
                    if u == 12:
                        top_two(FFN1, i + 1)

                s, _, f = ffn_of_b(i)
                slots(s, f, None, before_b(i), misc, residual)

            def split_part(n):
                dve.wait_ge(w_hi, n + 1)
                dve.tensor_tensor(part_lo[n], stage[:, n % 4, :], part_hi[n].bitcast(F32),
                                  ALU.subtract).then_inc(w_lo, 1)

            dve.wait_ge(x_loaded, 16)
            statistics(FFN1, 0, x0)
            layer_norm(FFN1, 0, x0)
            dve.wait_ge(ffn_loaded, 16 * 4)
            dve.tensor_copy(gwh[:, :], gwf[:, :]).then_inc(small_w, 1)
            dve.wait_ge(small_w, 1)
            dve.tensor_tensor(gwl[:, :], gwf[:, :], gwh[:, :].bitcast(F32), ALU.subtract).then_inc(small_w, 1)
            split_part(0)
            split_xT(FFN1, 0, O[:, :])
            split_part(1)
            dve.wait_ge(cst, 13)
            shift_logits(FFN1, 0, O[:, :])
            dve.tensor_copy(pick[:, :, :], hf[0:2 * E, 0:2, :].rearrange("k a t -> k (a t)")
                            .rearrange("k (e p) -> k e p", e=E)).then_inc(cst_dve, 1)
            probabilities(FFN1, 0)
            top_two(FFN1, 0)
            for k in range(2):
                first = DH * (1 + k)
                cols = ident[:, :].rearrange("p (g r) -> p g r", r=STEP)[:, :, first:first + DH]
                dve.tensor_reduce(lomask[:, k, :], cols, mybir.AxisListType.XY, ALU.add, negate=True).then_inc(cst_dve, 1)
            split_part(2)
            split_part(3)

            def attention_weights():
                dve.wait_ge(attn_loaded, 16 * 4)
                dve.tensor_scalar(wqkv_s, wqkv_s, gam[:, 0:1], None, ALU.mult).then_inc(small_step, 1)
                dve.memset(wqk_h[:, :, :, :].bitcast(F32), 0.0).then_inc(small_step, 1)
                dve.memset(wqk_l[:, :, :, :].bitcast(F32), 0.0).then_inc(small_step, 1)
                dve.wait_ge(small_step, 3)
                dve.tensor_scalar(wqkv_s[:, 0:D], wqkv_s[:, 0:D], float(DH) ** -0.5, None, ALU.mult).then_inc(small_step, 1)
                dve.wait_ge(small_step, 4)
                for k in range(2):
                    src = wqkv_s[:, k * D:k * D + D].rearrange("p (g h e) -> p g h e", h=2, e=DH)
                    hi, lo = (w[:, k, :, :].rearrange("p g (h r e) -> p g h r e", h=2, e=DH) for w in (wqk_h, wqk_l))
                    for r in range(3):
                        dve.tensor_copy(hi[:, :, :, r, :], src).then_inc(small_step, 1)
                        dve.wait_ge(small_step, 4 + 3 * k + r + 1)
                        dve.tensor_tensor(lo[:, :, :, r, :], src, hi[:, :, :, r, :].bitcast(F32),
                                          ALU.subtract).then_inc(small_w, 1)
                dve.tensor_copy(wvh[:, :], wqkv_s[:, 2 * D:3 * D]).then_inc(small_step, 1)
                dve.tensor_copy(woh[:, :], wo_s).then_inc(small_step, 1)
                dve.wait_ge(small_step, 12)
                dve.tensor_tensor(wvl[:, :], wqkv_s[:, 2 * D:3 * D], wvh[:, :].bitcast(F32), ALU.subtract).then_inc(small_w, 1)
                dve.tensor_tensor(wol[:, :], wo_s, woh[:, :].bitcast(F32), ALU.subtract).then_inc(small_w, 1)
                dve.wait_ge(small_w, 10)

            def first_misc(u):
                if u + 4 < len(parts):
                    split_part(u + 4)
                if u == 12:
                    attention_weights()

            def finish():
                f = ffn_number(FFN1, NB)
                gate_y(f, 6)
                split_h(FFN1, f, CHUNKS - 1)
                gate_y(f, 7)
                add_ffn2(f, x0)

            slots(FFN1, 0, None, None, first_misc, None)
            pipeline(dve, phase_a, phase_b, finish)


_INS = ["x", "gamma", "wq", "wkv", "wo", "gw", "gb", "w1", "b1", "w2", "b2"]


def kernel(L0_attn_x, L0_attn_gamma, L0_attn_w_q, L0_attn_w_kv, L0_attn_w_out, L0_ffn_gate_w, L0_ffn_gate_b,
           L0_ffn_w1, L0_ffn_b1, L0_ffn_w2, L0_ffn_b2):
    import numpy as _np
    import concourse.bacc as _bacc
    from concourse.bass_utils import run_bass_kernel_spmd as _run

    arrays = {
        "x": L0_attn_x,
        "gamma": _np.reshape(L0_attn_gamma, (D, 1)),
        "wq": L0_attn_w_q,
        "wkv": L0_attn_w_kv,
        "wo": L0_attn_w_out,
        "gw": _np.transpose(L0_ffn_gate_w),
        "gb": L0_ffn_gate_b,
        "w1": L0_ffn_w1,
        "b1": _np.transpose(_np.reshape(L0_ffn_b1, (E * KC, P))),
        "w2": L0_ffn_w2,
        "b2": _np.transpose(L0_ffn_b2),
    }
    arrays = {f"in_{k}": _np.ascontiguousarray(a) for k, a in arrays.items()}
    nc = _bacc.Bacc("TRN2", target_bir_lowering=False, num_devices=1)
    args = [nc.dram_tensor(f"in_{k}", arrays[f"in_{k}"].shape, F32, kind="ExternalInput").ap() for k in _INS]
    out = nc.dram_tensor("out", (NB, T, D), F32, kind="ExternalOutput").ap()
    macaron(nc, *args, out)
    r = _run(nc, [arrays], core_ids=[0])
    return r.results[0]["out"]
```

```python
from contextlib import ExitStack

import concourse.bass as bass
from concourse import mybir

F32 = mybir.dt.float32
F32R = mybir.dt.float32r
ALU = mybir.AluOpType
ACT = mybir.ActivationFunctionType
AX_X = mybir.AxisListType.X

P = 128
NB, T, D = 8, 512, 128
TC = T // P
E, H = 8, 512
KC = H // P
CHUNKS = E * KC
UNITS = CHUNKS // 2
GATES = 4
LAG = 4
HEADS, DH = 8, 16
VW = DH + 1
STEP = 64
LN_EPS, DEN_EPS, NORM_EPS = 1e-5, 1e-5, 1e-12
FFN1, FFN2 = 0, 1


def ffn_number(stage, j):
    if stage == FFN1:
        return 0 if isinstance(j, int) and j == 0 else j * 2 - 1
    return j * 2 + 2


def need(eng, sem=None, count=0):
    if not (isinstance(count, int) and count <= 0):
        eng.wait_ge(sem, count)


POOL_LO = (
    (0, 1, 2, 4, 5, 6, 7, 9, 10, 11, 12, 13, 14, 16, 17, 19, 20, 21, 23, 24, 26, 28, 30),
    (0, 1, 2, 4, 5, 6, 8, 9, 12, 13, 14, 16, 17, 18, 19, 20, 21, 22, 24, 25, 26, 28, 30),
)
DVE_HI = (0, 1, 2, 3, 4, 5, 6, 7, 8, 9, 11, 12, 13, 15)


def by_pool(s, c):
    return c in POOL_LO[s]


def lo_count(s, f, c):
    mine = [by_pool(s, x) == by_pool(s, c) for x in range(CHUNKS)]
    return f * sum(mine) + sum(mine[:c + 1])


def macaron(nc, x_d, gamma_d, wq_d, wkv_d, wo_d, gw_d, gb_d, w1_d, b1_d, w2_d, b2_d, out_d):
    with ExitStack() as ctx:
        def sb(name, shape, dt=F32):
            return ctx.enter_context(nc.sbuf_tensor(name, shape, dt))

        def pb(name, shape):
            return ctx.enter_context(nc.psum_tensor(name, shape, F32))

        def sem(name):
            return ctx.enter_context(nc.semaphore(name))

        w1h, w1l = sb("w1h", [P, E, H], F32R), sb("w1l", [P, E, H], F32R)
        w2h, w2l = sb("w2h", [P, E, KC, D], F32R), sb("w2l", [P, E, KC, D], F32R)
        b1c, b2c = sb("b1c", [P, E * KC]), sb("b2c", [P, E])
        gwf = sb("gwf", [P, E])
        gw_hl = sb("gw_hl", [P, 2, E], F32R)
        gbb = sb("gbb", [P, E])
        wqk_h, wqk_l = sb("wqk_h", [P, 2, P], F32R), sb("wqk_l", [P, 2, P], F32R)
        wvh, wvl = sb("wvh", [P, D], F32R), sb("wvl", [P, D], F32R)
        wo_hl = sb("wo_hl", [P, 2, D], F32R)
        gam = sb("gam", [P, 1])
        ident = sb("ident", [P, P])
        rank = sb("rank", [P, TC, E])
        ones = sb("ones", [P, P], F32R)
        onef, mhalf = sb("onef", [P, 1]), sb("mhalf", [P, TC])
        idle = sb("idle", [P, 1])
        x0, x1, x2 = sb("x0", [P, TC, D]), sb("x1", [P, TC, D]), sb("x2", [P, TC, D])
        xn = sb("xn", [P, TC, D])
        stats, mv = sb("stats", [P, TC, 6]), sb("mv", [P, TC, 2])
        rstd = sb("rstd", [P, TC])
        xTh = [sb(f"xTh{s}", [P, T], F32R) for s in range(2)]
        xTl = [sb(f"xTl{s}", [P, T], F32R) for s in range(2)]
        hf = sb("hf", [P, LAG, T])
        hh = sb("hh", [P, 2 * LAG, T], F32R)
        hl = sb("hl", [P, LAG, T], F32R)
        gate = sb("gate", [P, GATES, T])
        gy, acc = sb("gy", [P, T]), sb("acc", [P, T])
        lg, pr, pr2, tmp = (sb(n, [P, TC, E]) for n in ("lg", "pr", "pr2", "tmp"))
        f1, f2 = sb("f1", [P, TC, E]), sb("f2", [P, TC, E])
        red, rcp = sb("red", [P, TC]), sb("rcp", [P, TC])
        gates = [sb(f"gates{s}", [P, TC, E]) for s in range(2)]
        gTs = [sb(f"gTs{s}", [E, T]) for s in range(2)]
        nTh, nTl = sb("nTh", [P, T], F32R), sb("nTl", [P, T], F32R)
        qk_parts = sb("qk_parts", [P, 4, T], F32R)
        qk = sb("qk", [P, 2, 4, T], F32R)
        vp = sb("vp", [P, TC, HEADS * 2 * VW + P - 2 * VW], F32R)
        vps = vp[:, :, 0:HEADS * 2 * VW].rearrange("p c (h v) -> p c h v", v=2 * VW)
        vsum = sb("vsum", [P, HEADS, VW])
        Pf = sb("Pf", [P, 2, 2, T])
        Ph, Pl = sb("Ph", [P, 4, 2, T], F32R), sb("Pl", [P, 2, 2, T], F32R)
        osb = sb("osb", [2 * VW, 2, T])
        nsum, nrec = sb("nsum", [P, 2, TC, VW]), sb("nrec", [P, 2, TC, 1])
        on = sb("on", [P, TC, D])

        z = pb("z", [P, 2, T])
        y = pb("y", [P, 2, T])
        G = pb("G", [P, T])
        S = pb("S", [P, 2, T])
        O = pb("O", [P, T])

        x_loaded, w_loaded = sem("x_loaded"), [sem(f"w_loaded{k}") for k in range(4)]
        ffn_loaded, attn_loaded, stored = sem("ffn_loaded"), sem("attn_loaded"), sem("stored")
        zeroed, ident_ready = sem("zeroed"), sem("ident_ready")
        routing_cst, attn_cst = sem("routing_cst"), sem("attn_cst")
        w_hi, w_lo, small_w, small_step = sem("w_hi"), sem("w_lo"), sem("small_w"), sem("small_step")
        z_done, relu_done, h_hi = sem("z_done"), sem("relu_done"), sem("h_hi")
        h_lo = {True: sem("h_lo_pool"), False: sem("h_lo_dve")}
        y_part, gy_done, acc_done = sem("y_part"), sem("gy_done"), sem("acc_done")
        gate_loaded = [sem(f"gate_loaded{k}") for k in range(GATES)]
        accT_full, x1_ready, out_ready = sem("accT_full"), sem("x1_ready"), sem("out_ready")
        square_ready, rstd_ready = ([sem(f"{n}{s}") for s in range(3)] for n in ("square_ready", "rstd_ready"))
        floor_ready = sem("floor_ready")
        ln_step, xn_ready = [sem(f"ln_step{s}") for s in range(3)], [sem(f"xn_ready{s}") for s in range(3)]
        xT_full, xT_hi, xT_lo = ([sem(f"{n}{s}") for s in range(3)] for n in ("xT_full", "xT_hi", "xT_lo"))
        logit_full, shifted, exp_done, gate_step, gates_ready, gT_full, gT_ready = (
            [sem(f"{n}{s}") for s in range(2)] for n in
            ("logit_full", "shifted", "exp_done", "gate_step", "gates_ready", "gT_full", "gT_ready"))
        v_full, v_hi, v_lo, vsum_full, vsum_hi, vsum_ready = (
            sem(n) for n in ("v_full", "v_hi", "v_lo", "vsum_full", "vsum_hi", "vsum_ready"))
        qk_full, qk_hi, qk_lo = sem("qk_full"), sem("qk_hi"), sem("qk_lo")
        qk_moved = [sem(f"qk_moved{h}") for h in range(HEADS)]
        s_full, p_full, p_lo, pv_done = (sem(n) for n in ("s_full", "p_full", "p_lo", "pv_done"))
        p_hi = [sem("p_hi_scalar"), sem("p_hi_vector")]
        o_ready, oT_full, norm_step, norm_done = (sem(n) for n in ("o_ready", "oT_full", "norm_step", "norm_done"))
        onT_full, onT_hi, onT_lo, proj_full, x2_half, x2_ready = (
            sem(n) for n in ("onT_full", "onT_hi", "onT_lo", "proj_full", "x2_half", "x2_ready"))

        stage = Pf[:, :, :, :].rearrange("p a b t -> p (a b) t")
        parts = [(w, e) for e in range(E) for w in (1, 2)]
        part_hi = [w1h[:, e, :] if w == 1 else w2h[:, e, :, :].rearrange("p k d -> p (k d)") for w, e in parts]
        part_lo = [w1l[:, e, :] if w == 1 else w2l[:, e, :, :].rearrange("p k d -> p (k d)") for w, e in parts]
        wqkv_s = x1[:, :, :].rearrange("p c d -> p (c d)")[:, 0:3 * D]
        wo_s = x2[:, 0, :]
        NORM_STEPS = 4
        LN_STEPS = 2 * TC
        GATE_A, GATE_B = 11, 7

        def lo_ready(eng, s, f, c):
            if c < 0:
                f, c = f - 1, CHUNKS + c
            if not (isinstance(f, int) and f < 0):
                eng.wait_ge(h_lo[by_pool(s, c)], lo_count(s, f, c))

        block = ctx.enter_context(nc.Block())

        def pipeline(eng, phase_a, phase_b, finish):
            phase_b(0)
            phase_a(1)
            phase_b(1)
            with eng.Fori(2, NB - 1) as i:
                phase_a(i)
                phase_b(i)
            phase_a(NB - 1)
            phase_b(NB - 1)
            phase_a(NB)
            phase_b(NB)
            finish()

        def is_last(i):
            return isinstance(i, int) and i == NB

        def prepared(i):
            return (FFN1, NB) if is_last(i) else (FFN2, i - 1)

        def ffn_of_a(i):
            s, j = (FFN2, NB - 2) if is_last(i) else (FFN1, i)
            return s, j, ffn_number(s, j)

        def before_a(i):
            return None if isinstance(i, int) and (i < 2 or i == NB) else ffn_number(FFN2, i - 2)

        def late_gates(i):
            return isinstance(i, int) and i in (1, NB)

        def idle_b(i):
            return isinstance(i, int) and i in (0, NB - 1)

        def v_bank(i):
            return y[:, 0, :] if idle_b(i) else S[:, 0, :]

        def vsum_bank(i):
            return (y if idle_b(i) else S)[:, 1, 0:HEADS * 2 * VW]

        def ffn_of_b(i):
            s, j = prepared(i)
            return s, j, None if idle_b(i) else ffn_number(s, j)

        def before_b(i):
            return ffn_number(FFN2, NB - 2) if is_last(i) else ffn_number(FFN1, i)

        @block.sync
        def _(sp):
            def load_x(j):
                if not (isinstance(j, int) and j == 0):
                    need(sp, x1_ready, j)
                sp.dma_start(x0[:, :, :], x_d[j, :, :].rearrange("(p c) d -> p c d", c=TC)).then_inc(x_loaded, 16)

            def load_gate(s, j, f, e):
                used = f * E + e + 1 - GATES
                if e == 0:
                    if not isinstance(j, int):
                        used = sp.snap(used)
                    sp.wait_ge(gT_ready[s], j + 1)
                need(sp, gy_done, used)
                sp.dma_start(gate[:, e % GATES, :],
                             gTs[s][e:e + 1, :].unsqueeze(1).to_broadcast([1, P, T])
                             ).then_inc(gate_loaded[e % GATES], 16)

            load_x(0)
            sp.dma_start(gwf[:, :], gw_d).then_inc(ffn_loaded, 16)
            sp.dma_start(gbb[:, :], gb_d.partition_broadcast(P)).then_inc(ffn_loaded, 16)
            sp.dma_start(b1c[:, :], b1_d).then_inc(ffn_loaded, 16)
            sp.dma_start(b2c[:, :], b2_d).then_inc(ffn_loaded, 16)
            for n, (w, e) in enumerate(parts):
                need(sp, w_lo, n - 3)
                if w == 1:
                    sp.dma_start(stage[:, n % 4, :], w1_d[e, :, :]).then_inc(w_loaded[n % 4], 16)
                else:
                    sp.dma_start(stage[:, n % 4, :].rearrange("p (k d) -> p k d", k=KC),
                                 w2_d[e, :, :].rearrange("(k p) d -> p k d", p=P)).then_inc(w_loaded[n % 4], 16)
                if n in (9, 12, 14):
                    for e in {9: range(4), 12: (4,), 14: (5,)}[n]:
                        load_gate(FFN1, 0, 0, e)
                if n == 3:
                    sp.dma_start(gam[:, :], gamma_d).then_inc(attn_loaded, 16)
                    sp.dma_start(wqkv_s[:, 0:D], wq_d).then_inc(attn_loaded, 16)
                    sp.dma_start(wqkv_s[:, D:3 * D], wkv_d).then_inc(attn_loaded, 16)
                    sp.dma_start(wo_s, wo_d).then_inc(attn_loaded, 16)

            def store(j):
                sp.wait_ge(out_ready, j + 1)
                src = x0 if isinstance(j, int) and j == NB - 1 else x2
                sp.dma_start(out_d[j, :, :].rearrange("(p c) d -> p c d", c=TC), src[:, :, :]).then_inc(stored, 16)

            for e in (6, 7):
                load_gate(FFN1, 0, 0, e)

            def phase_a(i):
                for e in range(0 if is_last(i) else 2, 4):
                    load_gate(*ffn_of_a(i), e)
                if not (isinstance(i, int) and i in (1, NB)):
                    store(i - 2)
                for e in range(4, E):
                    load_gate(*ffn_of_a(i), e)

            def stack_heads(j):
                if isinstance(j, int) and j == 0:
                    sp.wait_ge(attn_cst, 4)
                sp.wait_ge(qk_lo, (j + 1) * 2)
                for h in range(HEADS):
                    src = qk_parts[h * DH:(h + 1) * DH, :, :]
                    for r, which in enumerate((slice(0, 4, 2), slice(1, 3), slice(0, 4, 3))):
                        row = STEP * (h % 2) + DH * r
                        sp.dma_start(qk[row:row + DH, :, h // 2, :].bitcast(F32),
                                     src[:, which, :].bitcast(F32)).then_inc(qk_moved[h], 16)

            def phase_b(i):
                ffn = None if idle_b(i) else ffn_of_b(i)
                for e in range(4 if ffn else 0):
                    load_gate(*ffn, e)
                if is_last(i):
                    store(NB - 2)
                elif not (isinstance(i, int) and i == NB - 1):
                    load_x(i + 1)
                for e in range(4, 7 if ffn else 0):
                    load_gate(*ffn, e)
                if not is_last(i):
                    stack_heads(i)
                if ffn:
                    load_gate(*ffn, 7)
                if not (isinstance(i, int) and i >= NB - 1):
                    for e in range(2):
                        load_gate(FFN1, i + 1, ffn_number(FFN1, i + 1), e)

            pipeline(sp, phase_a, phase_b, lambda: store(NB - 1))
            sp.wait_ge(stored, 16 * NB)

        @block.gpsimd
        def _(pool):
            pool.memset(mhalf[:, :], -0.5).then_inc(zeroed, 1)
            pool.memset(ident[:, :], 0.0).then_inc(zeroed, 1)
            pool.wait_ge(zeroed, 2)
            pool.affine_select(out=ident[:, :], in_=ident[:, :], compare_op=ALU.not_equal, fill=1.0, base=0,
                               pattern=[[-1, P]], channel_multiplier=1).then_inc(ident_ready, 1)

            def constants():
                for e in range(E):
                    pool.memset(rank[:, :, e:e + 1], float(E - e)).then_inc(routing_cst, 1)
                pool.memset(qk[:, :, :, :].bitcast(F32), 0.0).then_inc(attn_cst, 1)
                pool.memset(ones[:, :].bitcast(F32), 1.0).then_inc(attn_cst, 1)
                pool.memset(onef[:, :], 1.0).then_inc(attn_cst, 1)
                pool.memset(vp[:, :, :].bitcast(F32), 0.0).then_inc(zeroed, 1)
                pool.wait_ge(zeroed, 3)
                pool.memset(vps[:, :, :, DH:VW].bitcast(F32), 1.0).then_inc(attn_cst, 1)

            def split_h(s, f, c):
                pool.wait_ge(h_hi, f * CHUNKS + c + 1)
                need(pool, y_part, f * CHUNKS + c - LAG + 1)
                pool.tensor_tensor(hl[:, c % LAG, :], hf[:, c % LAG, :], hh[:, c % (2 * LAG), :].bitcast(F32),
                                   ALU.subtract).then_inc(h_lo[True], 1)

            def add_gated(f, e):
                pool.wait_ge(gy_done, f * 8 + e + 1)
                need(pool, acc_done, f * 7 + e - 1)
                pool.tensor_tensor(acc[:, :], acc[:, :], gy[:, :], ALU.add).then_inc(acc_done, 1)

            def inverse_deviation(s, j):
                pool.wait_ge(square_ready[s], j + 1)
                pool.tensor_tensor(rstd[:, :], rstd[:, :], mhalf[:, :], ALU.pow).then_inc(rstd_ready[s], 1)

            def slots(s, f, before, norms):
                for u in range(UNITS):
                    if u in norms:
                        inverse_deviation(*norms[u])
                    if before is not None and u in (0, 2):
                        add_gated(before, 6 + u // 2)
                    if f is not None:
                        if u >= 6 and u % 2 == 0:
                            add_gated(f, u // 2 - 2)
                        for c in (2 * u, 2 * u + 1):
                            if by_pool(s, c):
                                split_h(s, f, c)

            def phase_a(i):
                s, _, f = ffn_of_a(i)
                slots(s, f, before_a(i), {13: prepared(i)})

            def phase_b(i):
                s, _, f = ffn_of_b(i)
                norms = {} if is_last(i) else {5: (2, i)}
                if not (isinstance(i, int) and i >= NB - 1):
                    norms[8] = (FFN1, i + 1)
                slots(s, f, before_b(i), norms)

            inverse_deviation(FFN1, 0)
            constants()
            slots(FFN1, 0, None, {})
            pipeline(pool, phase_a, phase_b, lambda: slots(FFN1, None, ffn_number(FFN1, NB), {}))

        @block.scalar
        def _(act):
            def relu(s, f, u, cc):
                c = 2 * u + cc
                act.wait_ge(z_done, f * 32 + c + 1)
                lo_ready(act, s, f, c - LAG)
                act.activation(hf[:, c % LAG, :], z[:, c % 2, :], ACT.Relu,
                               bias=b1c[:, c:c + 1]).then_inc(relu_done, 1)

            def squares(j, p):
                act.wait_ge(s_full, j * 16 + p + 1)
                if p not in DVE_HI:
                    need(act, pv_done, j * 16 + p - 3)
                    act.activation(Ph[:, p % 4, :, :], S[:, :, :], ACT.Square, bias=onef[:, :]).then_inc(p_hi[0], 1)
                need(act, p_lo, j * 16 + p - 1)
                act.activation(Pf[:, p % 2, :, :], S[:, :, :], ACT.Square, bias=onef[:, :]).then_inc(p_full, 1)

            def head_out(j, h):
                act.wait_ge(pv_done, j * 16 + 2 * h + 2)
                need(act, oT_full, j * 4 + h // 2)
                act.activation(osb[:, h % 2, :], O[0:2 * VW, :], ACT.Copy).then_inc(o_ready, 1)

            def round_xT(s, j, bank):
                act.wait_ge(xT_full[s], j + 1)
                if s == 2:
                    need(act, proj_full, j)
                elif not (isinstance(j, int) and j == 0):
                    act.wait_ge(z_done, ffn_number(s, j - 1) * 32 + 32)
                dst = nTh if s == 2 else xTh[s]
                act.activation(dst[:, :], bank, ACT.Copy).then_inc(xT_hi[s], 1)

            def exps(s, j):
                act.wait_ge(shifted[s], j + 1)
                act.activation(tmp[:, :, :], lg[:, :, :], ACT.Exp).then_inc(exp_done[s], 1)

            def copy_gT(s, j, bank):
                act.wait_ge(gT_full[s], j + 1)
                if not (isinstance(j, int) and j == 0):
                    act.wait_ge(gy_done, ffn_number(s, j - 1) * E + E)
                act.activation(gTs[s][:, :], bank[0:E, :], ACT.Copy).then_inc(gT_ready[s], 1)

            def slots(s, f, heads, before, misc):
                for u in range(UNITS):
                    h = u - 1
                    if heads is not None and 0 <= h < HEADS:
                        squares(heads, 2 * h)
                    if f is not None:
                        relu(s, f, u, 0)
                    if heads is not None and 0 <= h < HEADS:
                        squares(heads, 2 * h + 1)
                    if f is not None:
                        relu(s, f, u, 1)
                    if heads is not None and 1 <= h <= HEADS:
                        head_out(heads, h - 1)
                    misc(u)

            def phase_a(i):
                def misc(u):
                    j = i - 1
                    if u == 2 and late_gates(i):
                        copy_gT(*ffn_of_a(i)[:2], G[:, :])
                    if u == 11:
                        act.wait_ge(onT_full, j + 1)
                        act.wait_ge(qk_full, (j + 1) * 2)
                        act.activation(nTh[:, :], S[:, 0, :], ACT.Copy).then_inc(onT_hi, 1)
                    if u == 14:
                        round_xT(*prepared(i), S[:, 0, :])
                    if u == 15:
                        exps(*prepared(i))

                s, _, f = ffn_of_a(i)
                slots(s, f, i - 1, before_a(i), misc)

            def phase_b(i):
                def misc(u):
                    if u == 2 and not idle_b(i):
                        copy_gT(*prepared(i), S[:, 1, :])
                    if is_last(i):
                        return
                    if u == 7:
                        round_xT(2, i, O[:, :])
                    if u == 9:
                        act.wait_ge(v_full, i + 1)
                        need(act, pv_done, i * 16)
                        act.activation(vps[:, :, :, 0:DH], v_bank(i).rearrange("p (c h e) -> p c h e", c=TC, h=HEADS),
                                       ACT.Copy).then_inc(v_hi, 1)
                    if u == 8:
                        for k in range(2):
                            act.wait_ge(qk_full, i * 2 + k + 1)
                            if k == 0:
                                for moved in qk_moved:
                                    need(act, moved, i * 48)
                            act.activation(qk_parts[:, 2 * k, :], S[:, k, :], ACT.Copy).then_inc(qk_hi, 1)
                    if isinstance(i, int) and i == NB - 1:
                        return
                    if u == 9:
                        round_xT(FFN1, i + 1, O[:, :])
                    if u == 10:
                        exps(FFN1, i + 1)
                    if u == 14 and not idle_b(i):
                        copy_gT(FFN1, i + 1, O[:, :])

                s, _, f = ffn_of_b(i)
                slots(s, f, None, before_b(i), misc)

            def round_part(n):
                act.wait_ge(w_loaded[n % 4], 16 * (n // 4 + 1))
                act.activation(part_hi[n], stage[:, n % 4, :], ACT.Copy).then_inc(w_hi, 1)

            def first_misc(u):
                if u == 0:
                    exps(FFN1, 0)
                if u == 2:
                    copy_gT(FFN1, 0, O[:, :])
                if u + 4 < len(parts):
                    round_part(u + 4)

            round_part(0)
            round_xT(FFN1, 0, O[:, :])
            for n in range(1, 4):
                round_part(n)
            act.wait_ge(ffn_loaded, 16 * 4)
            slots(FFN1, 0, None, None, first_misc)
            act.wait_ge(attn_cst, 4)
            act.wait_ge(w_lo, len(parts))
            pipeline(act, phase_a, phase_b, lambda: None)

        @block.tensor
        def _(pe):
            def three(out, a_hi, a_lo, b_hi, b_lo, start, stop):
                pe.matmul(out, a_hi, b_hi, start=start, stop=False)
                pe.matmul(out, a_hi, b_lo, start=False, stop=False)
                return pe.matmul(out, a_lo, b_hi, start=False, stop=stop)

            def three_wide(out, a_hi, a_lo, b_hl):
                half = b_hl.shape[2]
                pe.matmul(out, a_hi, b_hl, start=True, stop=False)
                return pe.matmul(out[:, 0:half], a_lo, b_hl[:, 0, :], start=False, stop=True)

            def mm1(s, f, u, cc):
                c = 2 * u + cc
                k = c % KC
                if isinstance(f, int) and f == 0 and cc == 0 and u % 2 == 0:
                    pe.wait_ge(w_lo, u + 1)
                need(pe, relu_done, f * 32 + c - 1)
                w = slice(k * P, k * P + P)
                three(z[:, c % 2, :], w1h[:, u // 2, w], w1l[:, u // 2, w], xTh[s][:, :], xTl[s][:, :],
                      True, True).then_inc(z_done, 1)

            def mm2(s, f, c):
                e, k = c // KC, c % KC
                if isinstance(f, int) and f == 0 and k == 0:
                    pe.wait_ge(w_lo, 2 * e + 2)
                lo_ready(pe, s, f, c)
                if k == 0:
                    need(pe, gy_done, f * 8 + e - 1)
                three(y[:, e % 2, :], w2h[:, e, k, :], w2l[:, e, k, :], hh[:, c % (2 * LAG), :], hl[:, c % LAG, :],
                      k == 0, k == KC - 1).then_inc(y_part, 1)

            def transpose_sum(f):
                pe.wait_ge(acc_done, f * 7 + 7)
                for c in range(TC):
                    mm = pe.transpose(G[:, c * P:c * P + P], acc[:, c * P:c * P + P], ident[:, :])
                mm.then_inc(accT_full, 1)

            def scores(j, p):
                h = p // 2
                if p % 2 == 0:
                    pe.wait_ge(qk_moved[h], (j + 1) * 48)
                if p == 0:
                    if not idle_b(j):
                        pe.wait_ge(vsum_ready, j + 1)
                else:
                    need(pe, p_full, j * 16 + p)
                rows = slice(STEP * (h % 2), STEP * (h % 2) + STEP)
                for mc in range(2):
                    m = 2 * (p % 2) + mc
                    mm = pe.matmul(S[:, mc, :], qk[rows, 1, h // 2, m * P:m * P + P], qk[rows, 0, h // 2, :],
                                   start=True, stop=True)
                mm.then_inc(s_full, 1)

            def weigh(j, p):
                h = p // 2
                pe.wait_ge(p_lo, j * 16 + p + 1)
                if p % 2 == 0:
                    need(pe, o_ready, j * 8 + h)
                for mc in range(2):
                    m = 2 * (p % 2) + mc
                    v = vp[:, m, h * 2 * VW:h * 2 * VW + P]
                    pe.matmul(O[:, :], v, Ph[:, p % 4, mc, :], start=(m == 0), stop=False)
                    mm = pe.matmul(O[:, :], v, Pl[:, p % 2, mc, :], start=False, stop=(m == TC - 1))
                mm.then_inc(pv_done, 1)

            def sum_values(j):
                pe.wait_ge(v_hi, j + 1)
                pe.wait_ge(v_lo, j + 1)
                for c in range(TC):
                    mm = pe.matmul(vsum_bank(j), ones[:, :], vp[:, c, 0:HEADS * 2 * VW],
                                   start=(c == 0), stop=(c == TC - 1))
                mm.then_inc(vsum_full, 1)

            def transpose_heads(j, hp, free):
                pe.wait_ge(o_ready, j * 8 + 2 * hp + 2)
                need(pe, *free)
                pe.matmul(G[:, 0:1], ident[:, :], ident[:, 0:1], start=True, stop=True)
                for h in range(2):
                    for c in range(TC):
                        at = (h * TC + c) * 2 * VW
                        mm = pe.transpose(G[:, at:at + 2 * VW], osb[:, h, c * P:c * P + P], ident[0:2 * VW, 0:2 * VW])
                mm.then_inc(oT_full, 1)

            def transpose_xn(s, j, bank):
                pe.wait_ge(xn_ready[s], j + 1)
                for c in range(TC):
                    mm = pe.transpose(bank[:, c * P:c * P + P], xn[:, c, :], ident[:, :])
                mm.then_inc(xT_full[s], 1)

            def logits(s, j, bank):
                pe.wait_ge(xT_hi[s], j + 1)
                pe.wait_ge(xT_lo[s], j + 1)
                for c in range(TC):
                    tok = slice(c * P, c * P + P)
                    mm = three_wide(bank[:, c * 2 * E:(c + 1) * 2 * E], xTh[s][:, tok], xTl[s][:, tok], gw_hl[:, :, :])
                mm.then_inc(logit_full[s], 1)

            def transpose_gates(s, j, bank):
                pe.wait_ge(gates_ready[s], j + 1)
                for c in range(TC):
                    mm = pe.transpose(bank[0:E, c * P:c * P + P], gates[s][:, c, :], ident[:, :])
                mm.then_inc(gT_full[s], 1)

            def slots(s, j, f, heads, before, residual, misc):
                for u in range(UNITS):
                    def second(cc):
                        c = 2 * u + cc - LAG
                        if c < 0:
                            if before is not None:
                                mm2(1 - s, before, CHUNKS + c)
                        elif f is not None:
                            mm2(s, f, c)

                    h = u - 1
                    if heads is not None and 0 <= h < HEADS:
                        scores(heads, 2 * h)
                    if f is not None:
                        mm1(s, f, u, 0)
                    second(0)
                    if u == 3 and before is not None:
                        transpose_sum(before)
                    if heads is not None and 4 <= u <= 10 and u % 2 == 0:
                        free = residual if u == 4 else (norm_done, heads * 4 + (u - 4) // 2)
                        transpose_heads(heads, (u - 4) // 2, free)
                    if heads is not None and 1 <= h <= HEADS:
                        weigh(heads, 2 * h - 2)
                    if heads is not None and 0 <= h < HEADS:
                        scores(heads, 2 * h + 1)
                    if f is not None:
                        mm1(s, f, u, 1)
                    misc(u)
                    second(1)
                    if heads is not None and 1 <= h <= HEADS:
                        weigh(heads, 2 * h - 1)

            def phase_a(i):
                def misc(u):
                    j = i - 1
                    if u == 0 and late_gates(i):
                        sum_values(j)
                    if u == 3 and late_gates(i):
                        pe.wait_ge(vsum_ready, j + 1)
                        s, tile, _ = ffn_of_a(i)
                        pe.wait_ge(gT_ready[s], tile + 1)
                    if u == 2 and late_gates(i):
                        transpose_gates(*ffn_of_a(i)[:2], G[:, :])
                    if u == 11:
                        pe.wait_ge(norm_done, j * 4 + 4)
                        pe.wait_ge(p_full, j * 16 + 16)
                        for c in range(TC):
                            mm = pe.transpose(S[:, 0, c * P:c * P + P], on[:, c, :], ident[:, :])
                        mm.then_inc(onT_full, 1)
                    if u == 12:
                        pe.wait_ge(onT_hi, j + 1)
                        pe.wait_ge(onT_lo, j + 1)
                        for c in range(TC):
                            tok = slice(c * P, c * P + P)
                            out = S[:, c // 2, c % 2 * 2 * D:(c % 2 + 1) * 2 * D]
                            mm = three_wide(out, nTh[:, tok], nTl[:, tok], wo_hl[:, :, :])
                        mm.then_inc(proj_full, 1)
                    if u == 14:
                        transpose_xn(*prepared(i), S[:, 0, :])
                    if u == 15:
                        logits(*prepared(i), S[:, 1, :])

                before = before_a(i)
                slots(*ffn_of_a(i), i - 1, before, () if before is None else (out_ready, i - 1), misc)

            def phase_b(i):
                def misc(u):
                    if u == 2 and not idle_b(i):
                        transpose_gates(*prepared(i), S[:, 1, :])
                    if is_last(i):
                        return
                    if u == 7:
                        need(pe, x2_ready, i)
                        transpose_xn(2, i, O[:, :])
                    if u == 8:
                        pe.wait_ge(xT_hi[2], i + 1)
                        pe.wait_ge(xT_lo[2], i + 1)
                        need(pe, shifted[FFN2] if idle_b(i) else gT_ready[FFN2], i)
                        for k in range(2):
                            three(S[:, k, :], wqk_h[:, k, :], wqk_l[:, k, :], nTh[:, :], nTl[:, :],
                                  True, True).then_inc(qk_full, 1)
                    if u == 9:
                        if idle_b(i):
                            pe.wait_ge(gy_done, before_b(i) * E + E)
                        else:
                            pe.wait_ge(qk_lo, i * 2 + 2)
                        for c in range(TC):
                            tok = slice(c * P, c * P + P)
                            mm = three(v_bank(i)[:, tok], nTh[:, tok], nTl[:, tok], wvh[:, :], wvl[:, :], True, True)
                        mm.then_inc(v_full, 1)
                    if u == 10 and not idle_b(i):
                        sum_values(i)
                    if isinstance(i, int) and i == NB - 1:
                        return
                    if u == 9:
                        transpose_xn(FFN1, i + 1, O[:, :])
                    if u == 10:
                        logits(FFN1, i + 1, O[:, :])
                    if u == 14 and not idle_b(i):
                        transpose_gates(FFN1, i + 1, O[:, :])

                slots(*ffn_of_b(i), None, before_b(i), (out_ready, NB - 1) if is_last(i) else (x1_ready, i + 1), misc)

            def finish():
                f = ffn_number(FFN1, NB)
                for u in range(2):
                    for cc in range(2):
                        mm2(FFN1, f, CHUNKS - LAG + 2 * u + cc)
                transpose_sum(f)

            def first_misc(u):
                if u == 0:
                    pe.wait_ge(small_w, 2)
                    logits(FFN1, 0, O[:, :])
                if u == 2:
                    transpose_gates(FFN1, 0, O[:, :])

            pe.wait_ge(ident_ready, 1)
            transpose_xn(FFN1, 0, O[:, :])
            pe.wait_ge(xT_hi[FFN1], 1)
            pe.wait_ge(xT_lo[FFN1], 1)
            slots(FFN1, 0, 0, None, None, (), first_misc)
            pe.wait_ge(attn_cst, 4)
            pe.wait_ge(small_w, 5)
            pipeline(pe, phase_a, phase_b, finish)

        @block.vector
        def _(dve):
            def bc(ap, n):
                return ap.unsqueeze(2).to_broadcast([P, TC, n])

            def split_h(s, f, c):
                dve.wait_ge(relu_done, f * CHUNKS + c + 1)
                need(dve, y_part, f * CHUNKS + c - 2 * LAG + 1)
                dve.tensor_copy(hh[:, c % (2 * LAG), :], hf[:, c % LAG, :]).then_inc(h_hi, 1)
                if not by_pool(s, c):
                    dve.wait_ge(h_hi, f * CHUNKS + c + 1)
                    need(dve, y_part, f * CHUNKS + c - LAG + 1)
                    dve.tensor_tensor(hl[:, c % LAG, :], hf[:, c % LAG, :], hh[:, c % (2 * LAG), :].bitcast(F32),
                                      ALU.subtract).then_inc(h_lo[False], 1)

            def gate_y(f, e):
                dve.wait_ge(y_part, f * CHUNKS + KC * (e + 1))
                dve.wait_ge(gate_loaded[e % GATES], (f * (E // GATES) + e // GATES + 1) * 16)
                if e == 0:
                    need(dve, accT_full, f)
                else:
                    need(dve, acc_done, f * 7 + e - 1)
                dve.scalar_tensor_tensor(acc[:, :] if e == 0 else gy[:, :], y[:, e % 2, :], b2c[:, e:e + 1],
                                         gate[:, e % GATES, :],
                                         ALU.add, ALU.mult).then_inc(gy_done, 1)

            def split_p(j, p):
                dve.wait_ge(p_full, j * 16 + p + 1)
                if p in DVE_HI:
                    need(dve, pv_done, j * 16 + p - 3)
                    dve.tensor_copy(Ph[:, p % 4, :, :], Pf[:, p % 2, :, :]).then_inc(p_hi[1], 1)
                    dve.wait_ge(p_hi[1], j * len(DVE_HI) + DVE_HI.index(p) + 1)
                need(dve, pv_done, j * 16 + p - 1)
                dve.tensor_tensor(Pl[:, p % 2, :, :], Pf[:, p % 2, :, :], Ph[:, p % 4, :, :].bitcast(F32),
                                  ALU.subtract).then_inc(p_lo, 1)

            def statistics(s, j, src):
                for c in range(TC):
                    dve.bn_stats(stats[:, c, :], src[:, c, :]).then_inc(ln_step[s], 1)
                dve.wait_ge(ln_step[s], j * LN_STEPS + TC)
                dve.memset(idle[:, :], 0.0)
                for c in range(TC):
                    dve.bn_aggr(mv[:, c, :], stats[:, c, :]).then_inc(ln_step[s], 1)

                dve.wait_ge(ln_step[s], (j + 1) * LN_STEPS)
                if s == 2:
                    dve.tensor_scalar(rstd[:, :], mv[:, :, 1], LN_EPS, NORM_EPS ** 2 / D,
                                      ALU.add, ALU.mult).then_inc(floor_ready, 1)
                    dve.wait_ge(floor_ready, j + 1)
                    dve.tensor_tensor(rstd[:, :], rstd[:, :], mv[:, :, 1], ALU.max).then_inc(square_ready[s], 1)
                else:
                    dve.tensor_scalar(rstd[:, :], mv[:, :, 1], LN_EPS, None, ALU.add).then_inc(square_ready[s], 1)

            def layer_norm(s, j, src):
                dve.wait_ge(rstd_ready[s], j + 1)
                if s == FFN1:
                    need(dve, xT_full[2], j)
                elif s == 2:
                    need(dve, xT_full[FFN2], j)
                    need(dve, xT_full[FFN1], j + 1)
                else:
                    need(dve, xT_full[FFN1], j + 2 if not (isinstance(j, int) and j == NB - 1) else NB)
                    need(dve, xT_full[2], j + 1)
                for c in range(TC):
                    ins = dve.tensor_scalar(xn[:, c, :], src[:, c, :], mv[:, c, 0:1], rstd[:, c:c + 1],
                                            ALU.subtract, ALU.mult)
                ins.then_inc(xn_ready[s], 1)

            def split_xT(s, j, bank):
                dve.wait_ge(xT_hi[s], j + 1)
                hi, lo = (nTh, nTl) if s == 2 else (xTh[s], xTl[s])
                dve.tensor_tensor(lo[:, :], bank, hi[:, :].bitcast(F32), ALU.subtract).then_inc(xT_lo[s], 1)

            def shift_logits(s, j, bank):
                n = j * (GATE_A + GATE_B)
                dve.wait_ge(logit_full[s], j + 1)
                halves = bank[:, 0:TC * 2 * E].rearrange("p (c e) -> p c e", e=2 * E)
                dve.tensor_tensor(pr2[:, :, :], halves[:, :, 0:E],
                                  gbb[:, :].unsqueeze(1).to_broadcast([P, TC, E]), ALU.add).then_inc(gate_step[s], 1)
                dve.wait_ge(gate_step[s], n + 1)
                dve.tensor_tensor(pr2[:, :, :], halves[:, :, E:2 * E], pr2[:, :, :], ALU.add).then_inc(gate_step[s], 1)
                n += 1
                dve.wait_ge(gate_step[s], n + 1)
                dve.tensor_reduce(red[:, :], pr2[:, :, :], AX_X, ALU.max).then_inc(gate_step[s], 1)
                dve.wait_ge(gate_step[s], n + 2)
                dve.tensor_tensor(lg[:, :, :], pr2[:, :, :], bc(red[:, :], E), ALU.subtract).then_inc(shifted[s], 1)

            def choose(s, n, values, out):
                dve.tensor_reduce(red[:, :], values[:, :, :], AX_X, ALU.max).then_inc(gate_step[s], 1)
                dve.wait_ge(gate_step[s], n + 1)
                dve.tensor_tensor(f2[:, :, :], values[:, :, :], bc(red[:, :], E),
                                  ALU.is_equal).then_inc(gate_step[s], 1)
                dve.wait_ge(gate_step[s], n + 2)
                dve.tensor_tensor(lg[:, :, :], f2[:, :, :], rank[:, :, :], ALU.mult).then_inc(gate_step[s], 1)
                dve.wait_ge(gate_step[s], n + 3)
                dve.tensor_reduce(red[:, :], lg[:, :, :], AX_X, ALU.max).then_inc(gate_step[s], 1)
                dve.wait_ge(gate_step[s], n + 4)
                dve.tensor_tensor(out[:, :, :], rank[:, :, :], bc(red[:, :], E), ALU.is_equal).then_inc(gate_step[s], 1)
                dve.wait_ge(gate_step[s], n + 5)

            def probabilities(s, j):
                n = j * (GATE_A + GATE_B) + 3
                dve.wait_ge(exp_done[s], j + 1)
                dve.tensor_reduce(red[:, :], tmp[:, :, :], AX_X, ALU.add).then_inc(gate_step[s], 1)
                dve.wait_ge(gate_step[s], n + 1)
                dve.reciprocal(rcp[:, :], red[:, :]).then_inc(gate_step[s], 1)
                dve.wait_ge(gate_step[s], n + 2)
                dve.tensor_tensor(pr[:, :, :], tmp[:, :, :], bc(rcp[:, :], E), ALU.mult).then_inc(gate_step[s], 1)
                dve.wait_ge(gate_step[s], n + 3)
                choose(s, n + 3, pr, f1)

            def top_two(s, j):
                n = j * (GATE_A + GATE_B) + GATE_A
                dve.scalar_tensor_tensor(pr2[:, :, :], f1[:, :, :], -2.0, pr[:, :, :],
                                         ALU.mult, ALU.add).then_inc(gate_step[s], 1)
                dve.wait_ge(gate_step[s], n + 1)
                choose(s, n + 1, pr2, tmp)
                dve.tensor_tensor(f1[:, :, :], f1[:, :, :], tmp[:, :, :], ALU.add).then_inc(gate_step[s], 1)
                dve.wait_ge(gate_step[s], n + 7)
                need(dve, gT_full[s], j)
                dve.tensor_tensor(gates[s][:, :, :], pr[:, :, :], f1[:, :, :], ALU.mult).then_inc(gates_ready[s], 1)

            def add_value_sums(j):
                dve.wait_ge(vsum_full, j + 1)
                sums = vsum_bank(j).rearrange("p (h v) -> p h v", v=2 * VW)
                dve.tensor_copy(vsum[:, :, :], sums[:, :, 0:VW]).then_inc(vsum_hi, 1)
                dve.wait_ge(vsum_hi, j + 1)
                dve.tensor_tensor(vsum[:, :, :], vsum[:, :, :], sums[:, :, VW:2 * VW], ALU.add).then_inc(vsum_ready, 1)

            def normalise(j, hp):
                n = (j * 4 + hp) * NORM_STEPS
                both = G[:, 0:4 * TC * VW].rearrange("p (h c v) -> p h c v", h=2, v=2 * VW)
                dve.wait_ge(oT_full, j * 4 + hp + 1)
                if hp == 0:
                    dve.wait_ge(vsum_ready, j + 1)
                dve.tensor_tensor(nsum[:, :, :, :], both[:, :, :, 0:VW],
                                  vsum[:, 2 * hp:2 * hp + 2, :].unsqueeze(2).to_broadcast([P, 2, TC, VW]),
                                  ALU.add).then_inc(norm_step, 1)
                dve.wait_ge(norm_step, n + 1)
                dve.tensor_tensor(nsum[:, :, :, :], nsum[:, :, :, :], both[:, :, :, VW:2 * VW],
                                  ALU.add).then_inc(norm_step, 1)
                dve.wait_ge(norm_step, n + 2)
                dve.tensor_scalar(nrec[:, :, :, :], nsum[:, :, :, DH:VW], 2 * DEN_EPS, None,
                                  ALU.max).then_inc(norm_step, 1)
                dve.wait_ge(norm_step, n + 3)
                dve.reciprocal(nrec[:, :, :, :], nrec[:, :, :, :]).then_inc(norm_step, 1)
                dve.wait_ge(norm_step, n + 4)
                if hp == 0:
                    need(dve, onT_full, j)
                ins = None
                for h in range(2):
                    head = 2 * hp + h
                    ins = dve.tensor_tensor(on[:, :, head * DH:head * DH + DH], nsum[:, h, :, 0:DH],
                                            nrec[:, h, :, :].to_broadcast([P, TC, DH]), ALU.mult)
                ins.then_inc(norm_done, 1)

            def slots(s, f, heads, before, misc, residual):
                for u in range(UNITS):
                    h = u - 1
                    if u in (0, 2) and before is not None:
                        gate_y(before, 6 + u // 2)
                    if u >= 4 and u % 2 == 0 and f is not None:
                        gate_y(f, u // 2 - 2)
                    if u > 0 and f is not None:
                        split_h(s, f, 2 * u - 1)
                    if u == 0 and before is not None:
                        split_h(1 - s, before, CHUNKS - 1)
                    if u == 3 and before is not None:
                        residual()
                    if heads is not None and 0 <= h < HEADS:
                        split_p(heads, 2 * h)
                    if f is not None:
                        split_h(s, f, 2 * u)
                    if heads is not None and 4 <= u <= 10 and u % 2 == 0:
                        normalise(heads, (u - 4) // 2)
                    if heads is not None and 0 <= h < HEADS:
                        split_p(heads, 2 * h + 1)
                    misc(u)

            def add_ffn2(f, x_in):
                dve.wait_ge(accT_full, f + 1)
                dve.scalar_tensor_tensor(x_in[:, :, :], G[:, :].rearrange("p (c d) -> p c d", c=TC), 0.5, x_in[:, :, :],
                                         ALU.mult, ALU.add).then_inc(out_ready, 1)

            def phase_a(i):
                x_in = x0 if is_last(i) else x2

                def misc(u):
                    j = i - 1
                    if u == 0 and late_gates(i):
                        add_value_sums(j)
                    if u == 11:
                        dve.wait_ge(onT_hi, j + 1)
                        dve.tensor_tensor(nTl[:, :], S[:, 0, :], nTh[:, :].bitcast(F32),
                                          ALU.subtract).then_inc(onT_lo, 1)
                    if u == 12:
                        dve.wait_ge(proj_full, j + 1)
                        if not (isinstance(i, int) and (i < 2 or i == NB)):
                            dve.wait_ge(stored, (i - 1) * 16)
                        halves = S[:, :, :].rearrange("p b (c d) -> p (b c) d", d=2 * D)
                        dve.tensor_tensor(x_in[:, :, :], halves[:, :, 0:D], x1[:, :, :], ALU.add).then_inc(x2_half, 1)
                        dve.wait_ge(x2_half, j + 1)
                        dve.tensor_tensor(x_in[:, :, :], halves[:, :, D:2 * D], x_in[:, :, :],
                                          ALU.add).then_inc(x2_ready, 1)
                        dve.wait_ge(x2_ready, j + 1)
                        statistics(*prepared(i), x_in)
                    if u == 13:
                        layer_norm(*prepared(i), x_in)
                    if u == 14:
                        split_xT(*prepared(i), S[:, 0, :])
                    if u == 15:
                        shift_logits(*prepared(i), S[:, 1, :])

                s, _, f = ffn_of_a(i)
                before = before_a(i)
                slots(s, f, i - 1, before, misc, lambda: add_ffn2(before, x2))

            def phase_b(i):
                def residual():
                    if is_last(i):
                        add_ffn2(before_b(i), x2)
                        return
                    dve.wait_ge(accT_full, ffn_number(FFN1, i) + 1)
                    dve.scalar_tensor_tensor(x1[:, :, :], G[:, :].rearrange("p (c d) -> p c d", c=TC), 0.5, x0[:, :, :],
                                             ALU.mult, ALU.add).then_inc(x1_ready, 1)

                def misc(u):
                    if u == (11 if idle_b(i) else 0) and not (isinstance(i, int) and i == 0):
                        probabilities(*prepared(i))
                    if u == (12 if idle_b(i) else 1) and not (isinstance(i, int) and i == 0):
                        top_two(*prepared(i))
                    if is_last(i):
                        return
                    if u == 4:
                        dve.wait_ge(x1_ready, i + 1)
                        statistics(2, i, x1)
                    if u == 6:
                        layer_norm(2, i, x1)
                    if u == 7:
                        split_xT(2, i, O[:, :])
                    if u == 9:
                        dve.wait_ge(v_hi, i + 1)
                        dve.tensor_tensor(vps[:, :, :, VW:VW + DH],
                                          v_bank(i).rearrange("p (c h e) -> p c h e", c=TC, h=HEADS),
                                          vps[:, :, :, 0:DH].bitcast(F32), ALU.subtract).then_inc(v_lo, 1)
                    if u == 10 and not idle_b(i):
                        add_value_sums(i)
                    if u == 8:
                        for k in range(2):
                            dve.wait_ge(qk_hi, i * 2 + k + 1)
                            dve.tensor_tensor(qk_parts[:, 2 * k + 1, :], S[:, k, :], qk_parts[:, 2 * k, :].bitcast(F32),
                                              ALU.subtract).then_inc(qk_lo, 1)
                    if isinstance(i, int) and i == NB - 1:
                        return
                    if u == 7:
                        dve.wait_ge(x_loaded, (i + 2) * 16)
                        statistics(FFN1, i + 1, x0)
                    if u == 8:
                        layer_norm(FFN1, i + 1, x0)
                    if u == 9:
                        split_xT(FFN1, i + 1, O[:, :])
                    if u == 10:
                        shift_logits(FFN1, i + 1, O[:, :])
                    if u == 11:
                        probabilities(FFN1, i + 1)
                    if u == 12:
                        top_two(FFN1, i + 1)

                s, _, f = ffn_of_b(i)
                slots(s, f, None, before_b(i), misc, residual)

            def split_part(n):
                dve.wait_ge(w_hi, n + 1)
                dve.tensor_tensor(part_lo[n], stage[:, n % 4, :], part_hi[n].bitcast(F32),
                                  ALU.subtract).then_inc(w_lo, 1)

            def attention_weights(n):
                if n == 0:
                    dve.wait_ge(attn_loaded, 16 * 4)
                    dve.tensor_scalar(wqkv_s, wqkv_s, gam[:, 0:1], None, ALU.mult).then_inc(small_step, 1)
                    dve.wait_ge(small_step, 1)
                    dve.tensor_scalar(wqkv_s[:, 0:D], wqkv_s[:, 0:D], float(DH) ** -0.5, None,
                                      ALU.mult).then_inc(small_step, 1)
                    dve.wait_ge(small_step, 2)
                elif n == 1:
                    src = wqkv_s[:, 0:2 * D].rearrange("p (k m) -> p k m", k=2)
                    dve.tensor_copy(wqk_h[:, :, :], src).then_inc(small_step, 1)
                    dve.wait_ge(small_step, 3)
                    dve.tensor_tensor(wqk_l[:, :, :], src, wqk_h[:, :, :].bitcast(F32), ALU.subtract).then_inc(small_w, 1)
                else:
                    dve.tensor_copy(wvh[:, :], wqkv_s[:, 2 * D:3 * D]).then_inc(small_step, 1)
                    dve.tensor_copy(wo_hl[:, 0, :], wo_s).then_inc(small_step, 1)
                    dve.wait_ge(small_step, 5)
                    dve.tensor_tensor(wvl[:, :], wqkv_s[:, 2 * D:3 * D], wvh[:, :].bitcast(F32),
                                      ALU.subtract).then_inc(small_w, 1)
                    dve.tensor_tensor(wo_hl[:, 1, :], wo_s, wo_hl[:, 0, :].bitcast(F32), ALU.subtract).then_inc(small_w, 1)
                    dve.wait_ge(small_w, 5)

            def first_misc(u):
                if u == 0:
                    shift_logits(FFN1, 0, O[:, :])
                    dve.wait_ge(routing_cst, E)
                    probabilities(FFN1, 0)
                if u == 1:
                    top_two(FFN1, 0)
                if u + 4 < len(parts):
                    split_part(u + 4)
                if 5 <= u < 8:
                    attention_weights(u - 5)

            dve.wait_ge(x_loaded, 16)
            statistics(FFN1, 0, x0)
            layer_norm(FFN1, 0, x0)
            dve.wait_ge(ffn_loaded, 16 * 4)
            dve.tensor_copy(gw_hl[:, 0, :], gwf[:, :]).then_inc(small_w, 1)
            dve.wait_ge(small_w, 1)
            dve.tensor_tensor(gw_hl[:, 1, :], gwf[:, :], gw_hl[:, 0, :].bitcast(F32), ALU.subtract).then_inc(small_w, 1)
            split_xT(FFN1, 0, O[:, :])
            split_part(0)
            split_part(1)
            split_part(2)
            split_part(3)

            def finish():
                f = ffn_number(FFN1, NB)
                gate_y(f, 6)
                split_h(FFN1, f, CHUNKS - 1)
                gate_y(f, 7)
                add_ffn2(f, x0)

            slots(FFN1, 0, None, None, first_misc, None)
            pipeline(dve, phase_a, phase_b, finish)


_INS = ["x", "gamma", "wq", "wkv", "wo", "gw", "gb", "w1", "b1", "w2", "b2"]


def kernel(L0_attn_x, L0_attn_gamma, L0_attn_w_q, L0_attn_w_kv, L0_attn_w_out, L0_ffn_gate_w, L0_ffn_gate_b,
           L0_ffn_w1, L0_ffn_b1, L0_ffn_w2, L0_ffn_b2):
    import numpy as _np
    import concourse.bacc as _bacc
    from concourse.bass_utils import run_bass_kernel_spmd as _run

    arrays = {
        "x": L0_attn_x,
        "gamma": _np.reshape(L0_attn_gamma, (D, 1)),
        "wq": L0_attn_w_q,
        "wkv": L0_attn_w_kv,
        "wo": L0_attn_w_out,
        "gw": _np.transpose(L0_ffn_gate_w),
        "gb": L0_ffn_gate_b,
        "w1": L0_ffn_w1,
        "b1": _np.transpose(_np.reshape(L0_ffn_b1, (E * KC, P))),
        "w2": L0_ffn_w2,
        "b2": _np.transpose(L0_ffn_b2),
    }
    arrays = {f"in_{k}": _np.ascontiguousarray(a) for k, a in arrays.items()}
    nc = _bacc.Bacc("TRN2", target_bir_lowering=False, num_devices=1)
    args = [nc.dram_tensor(f"in_{k}", arrays[f"in_{k}"].shape, F32, kind="ExternalInput").ap() for k in _INS]
    out = nc.dram_tensor("out", (NB, T, D), F32, kind="ExternalOutput").ap()
    macaron(nc, *args, out)
    r = _run(nc, [arrays], core_ids=[0])
    return r.results[0]["out"]
```
